# Optimizing a Trainium2 kernel written in Bass

```python
import numpy as np
import jax
import jax.numpy as jnp

def _softmax(x, axis=-1):
    return jax.nn.softmax(x, axis=axis)

def _gelu(x):
    return jax.nn.gelu(x, approximate=True)

def _silu(x):
    return jax.nn.silu(x)

def _sigmoid(x):
    return jax.nn.sigmoid(x)

def _layernorm(x, axis=-1, eps=1e-05):
    m = jnp.mean(x, axis=axis, keepdims=True)
    v = jnp.var(x, axis=axis, keepdims=True)
    return (x - m) / jnp.sqrt(v + eps)

def _scatter_add(tgt, idx, src, axis=0):
    return tgt.at[idx].add(src)

def _segment_sum(src, seg, n):
    return jax.ops.segment_sum(src, seg, n)
kernel_name = 'mk_lm_tower_d1_tok_ids2048_r4_fed445'

def setup_inputs(seed: int=0):
    np.random.seed(seed)
    _w = jnp.asarray

    def _rec_inputs():
        import jax
        import jax.numpy as jnp
        _rk = jax.random.key(seed)
        x = jax.random.randint(jax.random.fold_in(_rk, 1), (16, 512), 0, 8000, jnp.int32)
        return x
    x = _rec_inputs()

    def _L0_tok_setup():
        import jax, jax.numpy as jnp
        import numpy as np
        VOCAB = 8000
        DIM = 64
        key = jax.random.key(seed)
        k1, k2 = jax.random.split(key)
        sequence = jax.random.randint(k1, (16, 512), 0, VOCAB, dtype=jnp.int64 if jax.config.jax_enable_x64 else jnp.int32)
        weight = jax.random.normal(k2, (VOCAB, DIM), dtype=jnp.float32)
        return {'sequence': sequence, 'weight': weight}
    _L0_tok_all = _L0_tok_setup()
    _L0_tok_in = {k: v for k, v in _L0_tok_all.items() if k in ('weight',)}
    del _L0_tok_all

    def _L0_attn_setup():
        import jax, jax.numpy as jnp
        import numpy as np
        B, S, D, H = (4, 512, 512, 16)
        DH = D // H
        key = jax.random.key(seed)
        ks = jax.random.split(key, 11)
        p = 0.02
        return {'x': jax.random.normal(ks[0], (B, S, D), jnp.float32), 'Wq': jax.random.normal(ks[1], (D, D), jnp.float32) * p, 'bq': jax.random.normal(ks[2], (D,), jnp.float32) * p, 'Wk': jax.random.normal(ks[3], (D, D), jnp.float32) * p, 'bk': jax.random.normal(ks[4], (D,), jnp.float32) * p, 'Wv': jax.random.normal(ks[5], (D, D), jnp.float32) * p, 'bv': jax.random.normal(ks[6], (D,), jnp.float32) * p, 'Wo': jax.random.normal(ks[7], (D, D), jnp.float32) * p, 'bo': jax.random.normal(ks[8], (D,), jnp.float32) * p, 'spiral_weight': jax.random.normal(ks[9], (H,), jnp.float32), 'helix_rotation': jax.random.normal(ks[10], (D,), jnp.float32)}
    _L0_attn_all = _L0_attn_setup()
    _L0_attn_in = {k: v for k, v in _L0_attn_all.items() if k in ('Wq', 'bq', 'Wk', 'bk', 'Wv', 'bv', 'Wo', 'bo', 'spiral_weight', 'helix_rotation')}
    del _L0_attn_all

    def _L0_ffn_setup():
        import jax, jax.numpy as jnp
        import numpy as np
        FP8_MAX = 448.0
        SCALE_MARGIN = 0.8

        def _fp8_quant_dequant(t, scale):
            q = (t / scale).astype(jnp.float8_e4m3fn)
            return q.astype(jnp.float32) * scale
        key = jax.random.key(seed)
        k1, k2 = jax.random.split(key)
        B, S, D_IN, D_OUT = (4, 512, 512, 512)
        x = jax.random.normal(k1, (B, S, D_IN), dtype=jnp.float32)
        weight = jax.random.normal(k2, (D_OUT, D_IN), dtype=jnp.float32)
        bias = jnp.zeros((D_OUT,), dtype=jnp.float32)
        return {'x': x, 'weight': weight, 'bias': bias}
    _L0_ffn_all = _L0_ffn_setup()
    _L0_ffn_in = {k: v for k, v in _L0_ffn_all.items() if k in ('weight', 'bias')}
    del _L0_ffn_all
    return {'x': x, 'L0_tok_weight': _L0_tok_in['weight'], 'L0_attn_Wq': _L0_attn_in['Wq'], 'L0_attn_bq': _L0_attn_in['bq'], 'L0_attn_Wk': _L0_attn_in['Wk'], 'L0_attn_bk': _L0_attn_in['bk'], 'L0_attn_Wv': _L0_attn_in['Wv'], 'L0_attn_bv': _L0_attn_in['bv'], 'L0_attn_Wo': _L0_attn_in['Wo'], 'L0_attn_bo': _L0_attn_in['bo'], 'L0_attn_spiral_weight': _L0_attn_in['spiral_weight'], 'L0_attn_helix_rotation': _L0_attn_in['helix_rotation'], 'L0_ffn_weight': _L0_ffn_in['weight'], 'L0_ffn_bias': _L0_ffn_in['bias']}

def reference(x, L0_tok_weight, L0_attn_Wq, L0_attn_bq, L0_attn_Wk, L0_attn_bk, L0_attn_Wv, L0_attn_bv, L0_attn_Wo, L0_attn_bo, L0_attn_spiral_weight, L0_attn_helix_rotation, L0_ffn_weight, L0_ffn_bias):
    import jax
    import jax.numpy as jnp

    def _L0_tok_ref(sequence, weight):
        import jax, jax.numpy as jnp
        import numpy as np
        VOCAB = 8000
        DIM = 64
        embs = weight[sequence]
        bias = jnp.einsum('bsd,btd->bst', embs, embs) / jnp.sqrt(jnp.asarray(DIM, embs.dtype))
        return bias

    def _L0_attn_ref(x, Wq, bq, Wk, bk, Wv, bv, Wo, bo, spiral_weight, helix_rotation):
        import jax, jax.numpy as jnp
        import numpy as np
        B, S, D, H = (4, 512, 512, 16)
        DH = D // H
        b, s, d = x.shape
        h, dh = (H, d // H)
        q = (x @ Wq.T + bq).reshape(b, s, h, dh)
        k = (x @ Wk.T + bk).reshape(b, s, h, dh)
        v = (x @ Wv.T + bv).reshape(b, s, h, dh)
        rot = helix_rotation.reshape(h, dh)
        q = q * jnp.cos(rot)
        k = k * jnp.sin(rot)
        scores = jnp.einsum('bshd,bthd->bhst', q, k) / np.sqrt(dh).astype(np.float32)
        scores = scores * spiral_weight[None, :, None, None]
        attn = jax.nn.softmax(scores, axis=-1)
        out = jnp.einsum('bhst,bthd->bshd', attn, v).reshape(b, s, d)
        return out @ Wo.T + bo

    def _L0_ffn_ref(x, weight, bias):
        import jax, jax.numpy as jnp
        import numpy as np
        FP8_MAX = 448.0
        SCALE_MARGIN = 0.8

        def _fp8_quant_dequant(t, scale):
            q = (t / scale).astype(jnp.float8_e4m3fn)
            return q.astype(jnp.float32) * scale
        amax_x = jnp.max(jnp.abs(x))
        amax_w = jnp.max(jnp.abs(weight))
        x_scale = amax_x / (FP8_MAX * SCALE_MARGIN)
        w_scale = jnp.maximum(amax_x, amax_w) / (FP8_MAX * SCALE_MARGIN)
        x_scale = jax.lax.stop_gradient(x_scale)
        w_scale = jax.lax.stop_gradient(w_scale)
        x_dq = _fp8_quant_dequant(x, x_scale)
        w_dq = _fp8_quant_dequant(weight, w_scale)
        out = jnp.einsum('bsd,od->bso', x_dq, w_dq)
        return out + bias
    h = _L0_tok_ref(x, L0_tok_weight)
    h = h + _L0_attn_ref(_layernorm(h, axis=-1), L0_attn_Wq, L0_attn_bq, L0_attn_Wk, L0_attn_bk, L0_attn_Wv, L0_attn_bv, L0_attn_Wo, L0_attn_bo, L0_attn_spiral_weight, L0_attn_helix_rotation)
    h = h + _L0_ffn_ref(_layernorm(h, axis=-1), L0_ffn_weight, L0_ffn_bias)
    return h

_drawn_inputs = setup_inputs


def setup_inputs(seed=0):
    import zlib

    import numpy as np

    out = dict(_drawn_inputs(seed))
    spreads = {'L0_ffn_bias': (0.0, 0.8)}
    factors = {'L0_attn_Wq': 5.887,
     'L0_attn_bq': 8.0,
     'L0_attn_Wk': 5.779,
     'L0_attn_bk': 8.0,
     'L0_attn_Wv': 2.737,
     'L0_attn_bv': 2.885,
     'L0_attn_spiral_weight': 5.486,
     'L0_attn_helix_rotation': 5.771}
    for name, (base, spread) in spreads.items():
        noise = np.random.default_rng([zlib.crc32(name.encode()), seed]).standard_normal(out[name].shape)
        drawn = base * np.exp(spread * noise) if base else spread * noise
        out[name] = jnp.asarray(drawn.astype(out[name].dtype))
    for name, factor in factors.items():
        out[name] = (out[name] * factor).astype(out[name].dtype)
    return out
```

```python
from contextlib import ExitStack

import concourse.bass as bass
from concourse import mybir

ALU = mybir.AluOpType
ACT = mybir.ActivationFunctionType
AX_X = mybir.AxisListType.X
F32 = mybir.dt.float32
F32R = mybir.dt.float32r
BF16 = mybir.dt.bfloat16
I32 = mybir.dt.int32
U32 = mybir.dt.uint32

P = 128
B = 16
S = 512
E_DIM = 64
HEADS = 16
DH = S // HEADS
GH = 4
GROUPS = HEADS // GH
NT = S // P
STEPS = B * GROUPS
UNITS = GH * NT
AHEAD = 5
QK_ROWS = 3 * DH
QKM_ROWS = QK_ROWS + 2
EPS = 1e-5
FP8_RANGE = 448.0 * 0.8
MAGIC = 1.5 * 2.0 ** 23

MID = [(0, 0, "v0"), (0, 1, "pq"), (0, 3, "pk"), (0, 5, "v1"), (0, 7, "den"), (0, 9, "v2"), (0, 10, "v3"),
       (0, 12, "mt"), (0, 13, "wo0"), (0, 14, "wo1"), (0, 15, "wo2"),
       (1, 0, "wo3"), (1, 1, "pq"), (1, 2, "mean"), (1, 3, "pk"), (1, 4, "tu"), (1, 5, "h0_0"), (1, 6, "h0_1"),
       (1, 7, "den"), (1, 8, "h0_2"), (1, 9, "h0_3"), (1, 10, "aq"), (1, 12, "mt"), (1, 13, "tr"), (1, 14, "ak"),
       (2, 2, "pq"), (2, 4, "pk"), (2, 7, "den"), (2, 9, "av"), (2, 12, "mt"),
       (3, 1, "pq"), (3, 3, "pk"), (3, 7, "den"), (3, 12, "mt")]
PREPARE = ("mean", "tu", "h0_0", "h0_1", "h0_2", "h0_3", "aq", "tr", "ak", "av")
WO = ("wo0", "wo1", "wo2", "wo3")
FIRST = [x for x in MID if x[2] not in WO and x[::2] != (0, "den")]
LAST = [x for x in MID if x[2] not in PREPARE and not (x[0] >= 2 and x[2] in ("pq", "pk")) and x[::2] != (3, "mt")]
PROLOGUE = [(0, 0, n) for n in ("mean", "tu", "h0_0", "h0_1", "h0_2", "h0_3", "aq", "tr", "ak")] + [
    (0, 0, "pq"), (0, 0, "pk"), (1, 0, "pq"), (1, 0, "pk"), (0, 0, "av"), (0, 0, "mt")]
EPILOGUE = [(0, 0, "den")] + [(0, 0, n) for n in WO]
ITEMS = {"prologue": PROLOGUE, "first": FIRST, "mid": MID, "last": LAST, "epilogue": EPILOGUE}
HI = ("pq", "pk", "mt", "tu", "tr", "aq", "ak", "av")


def number(part, b, g, name, among=None):
    def size(p):
        return sum(1 for x in ITEMS[p] if among is None or x[2] in among)

    upto = [x[::2] for x in ITEMS[part]].index((g, name)) + 1
    here = sum(1 for x in ITEMS[part][:upto] if among is None or x[2] in among)
    if part == "prologue":
        return here
    if part == "first":
        return size("prologue") + here
    base = size("prologue") + size("first")
    if part == "mid":
        return base + (b - 1) * size("mid") + here
    base += (B - 2) * size("mid")
    return base + here if part == "last" else base + size("last") + here


def items_at(part, g, slot):
    return [n for gg, ss, n in ITEMS[part] if gg == g and ss == slot]


def for_batches(eng, body):
    body("first", 0, 0)
    with eng.Fori(0, (B - 2) // 2) as pair:
        b = eng.snap(pair * 2 + 1)
        body("mid", b, 1)
        body("mid", b + 1, 0)
    body("last", B - 1, 1)


def stand_alone(eng, sem):
    eng.sem_inc(sem, 1)


def attention_block(nc, d, xc_dram, stats):
    with ExitStack() as ctx:
        def sb(name, shape, dt=F32):
            return ctx.enter_context(nc.sbuf_tensor(name, shape, dt))

        def pb(name, shape):
            return ctx.enter_context(nc.psum_tensor(name, shape, F32))

        def sem(name):
            return ctx.enter_context(nc.semaphore(name))

        w_in = {n: sb(f"w_{n}", [P, NT, S]) for n in "qkv"}
        wo_hi, wo_lo = sb("wo_hi", [P, NT, S], F32R), sb("wo_lo", [P, NT, S], F32R)
        bq, bk, bv = sb("bq", [P, GROUPS]), sb("bk", [P, GROUPS]), sb("bv", [P, GROUPS])
        bo = sb("bo", [P, S])
        ones_mean = sb("ones_mean", [P, P])
        ones_den = sb("ones_den", [P, DH])
        ident = sb("ident", [P, P])
        q_stack = [sb(f"q_stack{g}", [P, GH, S], F32R) for g in range(GROUPS)]
        k_stack = [sb(f"k_stack{g}", [P, GH, S], F32R) for g in range(GROUPS)]
        q_hi, q_lo = sb("q_hi", [P, S], F32R), sb("q_lo", [P, S], F32R)
        k_hi, k_lo = sb("k_hi", [P, S], F32R), sb("k_lo", [P, S], F32R)
        v_sb = sb("v_sb", [P, NT, S])
        probs = sb("probs", [P, NT, GH, S])
        o_raw, o_sb = sb("o_raw", [P, S]), sb("o_sb", [P, S])
        o_hi, o_lo = sb("o_hi", [P, GROUPS, S], F32R), sb("o_lo", [P, GROUPS, S], F32R)
        h1 = sb("h1", [P, 2, S])
        xc = sb("xc", [P, 2, S])
        negmax = sb("negmax", [P, 2, NT, GH])
        m_parts = sb("m_parts", [DH + GH, S], F32R)
        ids = sb("ids", [P, NT], I32)
        emb = sb("emb", [P, NT, E_DIM])
        emb2 = sb("emb2", [P, NT, 2, E_DIM])
        cent2 = sb("cent2", [P, NT, 2, E_DIM])
        e_hi = [sb(f"e_hi{i}", [P, S], F32R) for i in range(2)]
        e_lo = [sb(f"e_lo{i}", [P, S], F32R) for i in range(2)]
        e_stk8 = [sb(f"e_stk8_{i}", [P, S], F32R) for i in range(2)]
        x_hi = sb("x_hi", [P, S], F32R)
        x_stk = sb("x_stk", [P, S], F32R)
        a_hi = {n: sb(f"a_hi_{n}", [P, S], F32R) for n in "qkv"}
        a_lo = {n: sb(f"a_lo_{n}", [P, S], F32R) for n in "qkv"}
        bn1, mv1 = sb("bn1", [P, NT, 6]), sb("mv1", [P, NT, 2])
        ve1, ln1v, y1, t1, r8 = (sb(n, [P, NT]) for n in ("ve1", "ln1v", "y1", "t1", "r8"))
        bn2, mv2, negm = sb("bn2", [P, 6]), sb("mv2", [P, NT, 3]), sb("negm", [P, NT])

        ps_s2 = pb("ps_s2", [P, 4, S])
        ps_s1 = pb("ps_s1", [P, 2, S])
        ps_d = pb("ps_d", [P, S])
        ps_o = pb("ps_o", [P, S])

        loaded = sem("loaded")
        wo_loaded = sem("wo_loaded")
        consts = sem("consts")
        pool_const = sem("pool_const")
        trig = sem("trig")
        trig_act = sem("trig_act")
        trig_dve = sem("trig_dve")
        w_ready = sem("w_ready")
        wo_ready = sem("wo_ready")
        ids_loaded = sem("ids_loaded")
        gathered = sem("gathered")
        emb2_ready = sem("emb2_ready")
        stk8_ready = sem("stk8_ready")
        xtop_ready = sem("xtop_ready")
        ln1 = sem("ln1")
        rsq = sem("rsq")
        dense_full = sem("dense_full")
        dense_done = sem("dense_done")
        hi_ready = sem("hi_ready")
        stack_loaded = sem("stack_loaded")
        m_loaded = sem("m_loaded")
        s1_full = sem("s1_full")
        max_done = sem("max_done")
        s2_full = sem("s2_full")
        exp_done = sem("exp_done")
        pv_done = sem("pv_done")
        added = sem("added")
        raw_copied = sem("raw_copied")
        rden = sem("rden")
        o_scaled = sem("o_scaled")
        ohi_done = sem("ohi_done")
        olo_done = sem("olo_done")
        ln2 = sem("ln2")
        xc_ready = sem("xc_ready")
        xc_stored = [sem(f"xc_stored{i}") for i in range(2)]

        dve_waited, pool_waited = sem("dve_waited"), sem("pool_waited")

        block = ctx.enter_context(nc.Block())

        wo_stage = probs[:, 0, :, :]
        L = S + GROUPS
        flat = probs[:, 1:4, :, :].rearrange("p a h n -> p (a h n)")

        def region(i):
            return flat[:, i * L:(i + 1) * L]

        rot, spiral, cosr, sinr, turn, red = (region(i) for i in range(6))
        bias_in = region(6)
        LOADS = 11

        @block.sync
        def _(sp):
            sp.dma_start(ids[:, :], d["ids"][0]).then_inc(ids_loaded, 16)
            sp.dma_start(rot[:, 0:S], d["rot_row"].partition_broadcast(P).rearrange("p a n -> p (a n)")).then_inc(loaded, 16)
            sp.dma_start(rot[:, S:L], d["rot_col"]).then_inc(loaded, 16)
            sp.dma_start(spiral[:, 0:S], d["spiral_row"].partition_broadcast(P).rearrange("p a n -> p (a n)")).then_inc(loaded, 16)
            sp.dma_start(spiral[:, S:L], d["spiral_col"]).then_inc(loaded, 16)
            sp.dma_start(bias_in[:, 0:GROUPS], d["bq_col"]).then_inc(loaded, 16)
            sp.dma_start(bias_in[:, GROUPS:2 * GROUPS], d["bk_col"]).then_inc(loaded, 16)
            for n in "qkv":
                sp.dma_start(w_in[n][:, :, :], d[f"w{n}"].rearrange("(t p) n -> p t n", p=P)).then_inc(loaded, 16)
            sp.dma_start(bv[:, :], d["bv_col"]).then_inc(loaded, 16)
            sp.dma_start(bo[:, :], d["bo_row"].partition_broadcast(P).rearrange("p a n -> p (a n)")).then_inc(loaded, 16)
            sp.dma_start(wo_stage, d["wo"].rearrange("(t p) n -> p t n", p=P)).then_inc(wo_loaded, 16)

            def load_ids(nb):
                sp.wait_ge(gathered, 16 * NT * nb)
                sp.dma_start(ids[:, :], d["ids"][nb]).then_inc(ids_loaded, 16)

            def stack_q(part, b, g, k, slot):
                sp.wait_ge(hi_ready, number(part, b, g, "pq", HI))
                sp.dma_start(q_stack[slot][0:DH, :, :].bitcast(F32), q_hi[:, :].bitcast(F32)).then_inc(stack_loaded, 16)
                sp.dma_start(q_stack[slot][2 * DH:3 * DH, :, :].bitcast(F32), q_hi[:, :].bitcast(F32)).then_inc(stack_loaded, 16)
                sp.wait_ge(dense_done, number(part, b, g, "pq"))
                sp.dma_start(q_stack[slot][DH:2 * DH, :, :].bitcast(F32), q_lo[:, :].bitcast(F32)).then_inc(stack_loaded, 16)

            def stack_k(part, b, g, k, slot):
                sp.wait_ge(hi_ready, number(part, b, g, "pk", HI))
                sp.dma_start(k_stack[slot][0:DH, :, :].bitcast(F32), k_hi[:, :].bitcast(F32)).then_inc(stack_loaded, 16)
                sp.dma_start(k_stack[slot][DH:2 * DH, :, :].bitcast(F32), k_hi[:, :].bitcast(F32)).then_inc(stack_loaded, 16)
                sp.wait_ge(dense_done, number(part, b, g, "pk"))
                sp.dma_start(k_stack[slot][2 * DH:3 * DH, :, :].bitcast(F32), k_lo[:, :].bitcast(F32)).then_inc(stack_loaded, 16)

            def max_rows(part, b, g, slot):
                sp.wait_ge(hi_ready, number(part, b, g, "mt", HI))
                sp.dma_start(q_stack[slot][QK_ROWS:QK_ROWS + 1, :, :].bitcast(F32), m_parts[0:GH, :].bitcast(F32)).then_inc(m_loaded, 16)
                sp.wait_ge(dense_done, number(part, b, g, "mt"))
                sp.dma_start(q_stack[slot][QK_ROWS + 1:QKM_ROWS, :, :].bitcast(F32), m_parts[DH:DH + GH, :].bitcast(F32)).then_inc(m_loaded, 16)

            def store_xc(pb_, st):
                sp.wait_ge(xc_ready, NT * pb_ + st + 1)
                sp.dma_start(xc_dram[pb_, st], xc[:, st % 2, :]).then_inc(xc_stored[st % 2], 16)

            stack_q("prologue", 0, 0, 0, 0)
            stack_k("prologue", 0, 0, 0, 0)
            stack_q("prologue", 0, 1, 1, 1)
            stack_k("prologue", 0, 1, 1, 1)
            max_rows("prologue", 0, 0, 0)

            def batch(part, b, parity):
                for g in range(GROUPS):
                    has = [n for gg, _, n in ITEMS[part] if gg == g]
                    if g == 0 and part != "last":
                        load_ids(b + 1)
                    if g == 1 and part != "first":
                        store_xc(b - 1, 2)
                    if "pq" in has:
                        stack_q(part, b, g, 4 * b + g + 2, (g + 2) % GROUPS)
                    if g == 1 and part != "first":
                        store_xc(b - 1, 3)
                    if "pk" in has:
                        stack_k(part, b, g, 4 * b + g + 2, (g + 2) % GROUPS)
                    if "mt" in has:
                        max_rows(part, b, g, (g + 1) % GROUPS)
                    if g == 0 and part != "first":
                        store_xc(b - 1, 0)
                        store_xc(b - 1, 1)

            for_batches(sp, batch)
            for st in range(NT):
                store_xc(B - 1, st)
            for i in range(2):
                sp.wait_ge(xc_stored[i], 16 * B * NT // 2)

        @block.tensor
        def _(pe):
            def open_dense(part, b, g, name):
                n = number(part, b, g, name)
                if not (isinstance(n, int) and n == 1):
                    pe.wait_ge(dense_done, n - 1)

            def mean(nb):
                pe.wait_ge(gathered, 16 * NT * (nb + 1))
                for tt in range(NT):
                    last = pe.matmul(ps_d[:, 0:E_DIM], ones_mean[:, :], emb[:, tt, :], start=(tt == 0), stop=(tt == NT - 1))
                last.then_inc(dense_full, 1)

            def turn_e(nb, scaled):
                if not scaled:
                    pe.wait_ge(emb2_ready, nb + 1)
                else:
                    pe.wait_ge(ln1, 10 * (nb + 1))
                for tt in range(NT):
                    last = pe.transpose(ps_d[:, tt * P:(tt + 1) * P], emb2[:, tt, :, :].rearrange("p c e -> p (c e)"), ident[:, :])
                last.then_inc(dense_full, 1)

            def h0_rows(nb, par, st):
                if st == 0:
                    pe.wait_ge(stk8_ready, 2 * (nb + 1))
                w = e_stk8[par][:, st * P:(st + 1) * P]
                pe.matmul(ps_d[:, :], w, e_hi[par][:, :], start=True, stop=False)
                pe.matmul(ps_d[:, :], w, e_lo[par][:, :], start=False, stop=True).then_inc(dense_full, 1)

            def make_a(n):
                for jt in range(NT):
                    last = pe.matmul(ps_d[:, :], cent2[:, jt, :, :].rearrange("p c e -> p (c e)"), w_in[n][:, jt, :],
                                     start=(jt == 0), stop=(jt == NT - 1))
                last.then_inc(dense_full, 1)

            def project(n, nb, g):
                pe.wait_ge(xtop_ready, nb + 1)
                pe.matmul(ps_d[:, :], a_hi[n][:, g * P:(g + 1) * P], x_stk[:, :], start=True, stop=False)
                pe.matmul(ps_d[:, :], a_lo[n][:, g * P:(g + 1) * P], x_stk[:, :], start=False, stop=True).then_inc(dense_full, 1)

            def project_v(tt):
                w = x_stk[:, tt * P:(tt + 1) * P]
                pe.matmul(ps_d[:, :], w, a_hi["v"][:, :], start=True, stop=False)
                pe.matmul(ps_d[:, :], w, a_lo["v"][:, :], start=False, stop=True).then_inc(dense_full, 1)

            def turn_max(k, g):
                pe.wait_ge(max_done, UNITS * (k + 1))
                for st in range(NT):
                    last = pe.transpose(ps_d[0:GH, st * P:(st + 1) * P], negmax[:, g % 2, st, :], ident[:, :])
                last.then_inc(dense_full, 1)

            def denominators(k):
                pe.wait_ge(added, 3 * (k + 1))
                for j in range(GH):
                    last = pe.matmul(ps_d[j * DH:(j + 1) * DH, :], ones_den[:, :], probs[:, NT - 1, j, :], start=True, stop=True)
                last.then_inc(dense_full, 1)

            def out_proj(pb_, par, st):
                if st == 0:
                    pe.wait_ge(olo_done, GROUPS * (pb_ + 1))
                w = e_stk8[par][:, st * P:(st + 1) * P]
                pe.matmul(ps_d[:, :], w, e_hi[par][:, :], start=True, stop=False)
                pe.matmul(ps_d[:, :], w, e_lo[par][:, :], start=False, stop=False)
                for c in range(NT):
                    pe.matmul(ps_d[:, :], o_hi[:, c, st * P:(st + 1) * P], wo_hi[:, c, :], start=False, stop=False)
                    pe.matmul(ps_d[:, :], o_hi[:, c, st * P:(st + 1) * P], wo_lo[:, c, :], start=False, stop=False)
                    last = pe.matmul(ps_d[:, :], o_lo[:, c, st * P:(st + 1) * P], wo_hi[:, c, :], start=False, stop=(c == NT - 1))
                last.then_inc(dense_full, 1)

            def scores_st(k, g, u, first):
                if u == 0:
                    pe.wait_ge(stack_loaded, 96 * (k + 1))
                if not (first and u < 2):
                    pe.wait_ge(max_done, UNITS * k + u - 1)
                j, st = u // NT, u % NT
                pe.matmul(ps_s1[:, u % 2, :], q_stack[g][0:QK_ROWS, j, st * P:(st + 1) * P], k_stack[g][0:QK_ROWS, j, :],
                          start=True, stop=True).then_inc(s1_full, 1)

            def scores_ts(k, g, i, first):
                if i == 0:
                    pe.wait_ge(m_loaded, 32 * (k + 1))
                if i % 2 == 0 and not (first and i < 4):
                    pe.wait_ge(exp_done, 8 * k + i // 2 - 1)
                tt, j = i // GH, i % GH
                ins = pe.matmul(ps_s2[:, i % 4, :], k_stack[g][0:QKM_ROWS, j, tt * P:(tt + 1) * P], q_stack[g][0:QKM_ROWS, j, :],
                                start=True, stop=True)
                if i % 2 == 1:
                    ins.then_inc(s2_full, 1)

            def times_v(k, g, tt, first, part=None, b=None):
                pe.wait_ge(exp_done, 8 * k + 2 * tt + 2)
                if g == 0:
                    pe.wait_ge(dense_done, number(part, b, 0, f"v{tt}"))
                if tt == 0 and not first:
                    pe.wait_ge(raw_copied, k)
                for j in range(GH):
                    h = g * GH + j
                    last = pe.matmul(ps_o[j * DH:(j + 1) * DH, :], v_sb[:, tt, h * DH:(h + 1) * DH], probs[:, tt, j, :],
                                     start=(tt == 0), stop=(tt == NT - 1), skip_group_check=True)
                last.then_inc(pv_done, 1)

            def dense(part, b, parity, g, name):
                open_dense(part, b, g, name)
                nb, npar = (0, 0) if part == "prologue" else (b + 1, 1 - parity)
                if name == "mean":
                    mean(nb)
                elif name == "tu":
                    turn_e(nb, False)
                elif name == "tr":
                    turn_e(nb, True)
                elif name.startswith("h0_"):
                    h0_rows(nb, npar, int(name[3]))
                elif name in ("aq", "ak", "av"):
                    make_a(name[1])
                elif name in ("pq", "pk"):
                    if part == "prologue":
                        project(name[1], 0, g)
                    else:
                        project(name[1], b + (g + 2) // GROUPS, (g + 2) % GROUPS)
                elif name[0] == "v":
                    project_v(int(name[1]))
                elif name == "mt":
                    turn_max(0 if part == "prologue" else GROUPS * b + g + 1, 0 if part == "prologue" else (g + 1) % GROUPS)
                elif name == "den":
                    denominators(STEPS - 1 if part == "epilogue" else GROUPS * b + g - 1)
                else:
                    out_proj(B - 1 if part == "epilogue" else b - 1, 1 if part == "epilogue" else 1 - parity, int(name[2]))

            pe.wait_ge(consts, 3)
            pe.wait_ge(pool_const, 2)
            for g, _, name in PROLOGUE:
                if name == "aq":
                    pe.wait_ge(w_ready, 2)
                if name == "av":
                    for u in range(UNITS):
                        scores_st(0, 0, u, True)
                dense("prologue", 0, 0, g, name)
            pe.wait_ge(wo_ready, 2)
            for u in range(AHEAD):
                scores_st(1, 1, u, False)

            def batch(part, b, parity):
                for g in range(GROUPS):
                    k = GROUPS * b + g
                    for i in range(UNITS):
                        for name in items_at(part, g, i):
                            dense(part, b, parity, g, name)
                        u = i + AHEAD
                        if u < UNITS and not (part == "last" and g + 1 >= GROUPS):
                            scores_st(k + 1, (g + 1) % GROUPS, u, False)
                        if u >= UNITS and not (part == "last" and g + 2 >= GROUPS):
                            scores_st(k + 2, (g + 2) % GROUPS, u - UNITS, False)
                        scores_ts(k, g, i, part == "first" and g == 0)
                        if i == 1 and not (part == "first" and g == 0):
                            times_v(k - 1, g - 1 if g else GROUPS - 1, NT - 1, False, part, b)
                        if i in (5, 9, 13):
                            times_v(k, g, (i - 5) // 4, part == "first" and g == 0, part, b)

            for_batches(pe, batch)
            times_v(STEPS - 1, GROUPS - 1, NT - 1, False)
            for g, _, name in EPILOGUE:
                dense("epilogue", B - 1, 1, g, name)

        @block.scalar
        def _(act):
            act.wait_ge(trig, 1)
            act.activation(cosr, cosr, ACT.Sin).then_inc(trig_act, 1)
            act.wait_ge(trig, 2)
            act.activation(sinr, sinr, ACT.Sin).then_inc(trig_act, 1)
            act.wait_ge(wo_loaded, 16)
            act.copy(wo_hi[:, :, :], wo_stage).then_inc(wo_ready, 1)

            def hi(part, b, g, name, out, bias=None):
                act.wait_ge(dense_full, number(part, b, g, name))
                src = ps_d[0:out.shape[0], :]
                if bias is None:
                    act.copy(out, src).then_inc(hi_ready, 1)
                else:
                    act.activation(out, src, ACT.Identity, bias=bias).then_inc(hi_ready, 1)

            def dense(part, b, parity, g, name):
                nb, npar = (0, 0) if part == "prologue" else (b + 1, 1 - parity)
                if name in ("pq", "pk"):
                    gg = g if part == "prologue" else (g + 2) % GROUPS
                    kk = g if part == "prologue" else GROUPS * b + g + 2
                    if not (part == "prologue" and g == 0):
                        act.wait_ge(stack_loaded, 96 * kk)
                    out, bias = (q_hi, bq) if name == "pq" else (k_hi, bk)
                    hi(part, b, g, name, out[:, :], bias[:, gg:gg + 1])
                elif name == "tu":
                    hi(part, b, g, name, e_hi[npar][:, :])
                elif name == "tr":
                    if part != "prologue":
                        act.wait_ge(xtop_ready, nb)
                    hi(part, b, g, name, x_hi[:, :])
                elif name in ("aq", "ak", "av"):
                    hi(part, b, g, name, a_hi[name[1]][:, :])
                elif name == "mt":
                    if part != "prologue":
                        act.wait_ge(m_loaded, 32 * (GROUPS * b + g + 1))
                    hi(part, b, g, name, m_parts[0:GH, :])
                elif name[0] == "v":
                    tt = int(name[1])
                    if part != "first":
                        act.wait_ge(pv_done, NT * GROUPS * b - NT + tt + 1)
                    act.wait_ge(dense_full, number(part, b, g, name))
                    act.copy(v_sb[:, tt, :], ps_d[:, :]).then_inc(dense_done, 1)
                elif name == "den":
                    inverse_den(part, b, g)

            def inverse_den(part, b, g):
                k = STEPS - 1 if part == "epilogue" else GROUPS * b + g - 1
                if not (isinstance(k, int) and k == 0):
                    act.wait_ge(olo_done, k)
                act.wait_ge(dense_full, number(part, b, g, "den"))
                act.activation(o_sb[:, :], ps_d[:, :], ACT.Ln).then_inc(dense_done, 1)
                act.wait_ge(dense_done, number(part, b, g, "den"))
                act.activation(o_sb[:, :], o_sb[:, :], ACT.Exp, scale=-1.0).then_inc(rden, 1)

            def rsqrt(nb):
                act.wait_ge(ln1, 10 * nb + 5)
                act.activation(ln1v[:, :], ve1[:, :], ACT.Ln).then_inc(rsq, 1)
                act.wait_ge(rsq, 2 * nb + 1)
                act.activation(y1[:, :], ln1v[:, :], ACT.Exp, scale=-0.5).then_inc(rsq, 1)

            def copy_raw(k, first):
                act.wait_ge(pv_done, NT * (k + 1))
                if not first:
                    act.wait_ge(o_scaled, k)
                act.copy(o_raw[:, :], ps_o[:, :]).then_inc(raw_copied, 1)

            def o_hi_part(part, b, g, k, gk):
                act.wait_ge(o_scaled, k + 1)
                if g == 1 and part in ("mid", "last"):
                    act.wait_ge(dense_full, number(part, b, 1, "wo3"))
                act.activation(o_hi[:, gk, :], o_sb[:, :], ACT.Identity, bias=bv[:, gk:gk + 1]).then_inc(ohi_done, 1)

            def center(pb_, st):
                act.wait_ge(ln2, 17 * pb_ + 4 * st + 3)
                n = NT * pb_ + st
                if not (isinstance(n, int) and n < 2):
                    act.wait_ge(xc_stored[st % 2], 16 * (NT // 2 * pb_ + st // 2))
                act.activation(xc[:, st % 2, :], h1[:, st % 2, :], ACT.Identity, bias=negm[:, st:st + 1]).then_inc(xc_ready, 1)

            def exp_pair(k, i, first):
                tt, jp = i // GH, (i % GH) // 2
                act.wait_ge(s2_full, 8 * k + i // 2 + 1)
                if jp == 0 and tt < NT - 1 and not first:
                    act.wait_ge(added, 3 * (k - 1) + tt + 1)
                act.activation(probs[:, tt, 2 * jp:2 * jp + 2, :], ps_s2[:, 2 * jp:2 * jp + 2, :], ACT.Exp).then_inc(exp_done, 1)

            for g, _, name in PROLOGUE:
                dense("prologue", 0, 0, g, name)
                if name == "h0_3":
                    rsqrt(0)

            def batch(part, b, parity):
                for g in range(GROUPS):
                    k = GROUPS * b + g
                    start = part == "first" and g == 0
                    for i in range(UNITS):
                        for name in items_at(part, g, i):
                            dense(part, b, parity, g, name)
                        if i == 3 and not start:
                            copy_raw(k - 1, part == "first" and g == 1)
                        if i == 9 and not start:
                            o_hi_part(part, b, g, k - 1, g - 1 if g else GROUPS - 1)
                        if g == 1 and i == 10 and part != "last":
                            rsqrt(b + 1)
                        if part != "first":
                            for st, at in enumerate(((0, 14), (0, 15), (1, 0), (1, 1))):
                                if at == (g, i):
                                    center(b - 1, st)
                        if i % 2:
                            exp_pair(k, i, start)

            act.wait_ge(w_ready, 2)
            act.wait_ge(wo_ready, 2)
            for_batches(act, batch)
            copy_raw(STEPS - 1, False)
            inverse_den("epilogue", B - 1, 0)
            o_hi_part("epilogue", B - 1, 0, STEPS - 1, GROUPS - 1)
            for st in range(NT):
                center(B - 1, st)

        @block.vector
        def _(dve):
            dve.memset(ones_mean[:, :], 1.0 / S).then_inc(consts, 1)
            dve.memset(ones_den[:, :], 1.0).then_inc(consts, 1)
            for g in range(GROUPS):
                last = dve.memset(k_stack[g][QK_ROWS:QKM_ROWS, :, :].bitcast(F32), 1.0)
            last.then_inc(consts, 1)

            dve.wait_ge(loaded, 16 * LOADS)
            two_pi = 6.283185307179586
            c1 = 6.28125
            c2 = 507.0 / 2 ** 18
            c3 = two_pi - c1 - c2
            chain = [0]

            def link(ins):
                chain[0] += 1
                ins.then_inc(trig_dve, 1)
                dve.wait_ge(trig_dve, chain[0])

            for out, phase, shift in ((cosr, 0.25, two_pi / 4), (sinr, 0.0, 0.0)):
                link(dve.tensor_scalar(turn, rot, 1.0 / two_pi, phase, ALU.mult, ALU.add))
                link(dve.tensor_scalar(red, turn, MAGIC, None, ALU.add))
                link(dve.tensor_scalar(turn, red, MAGIC, None, ALU.subtract))
                link(dve.scalar_tensor_tensor(red, turn, -c1, rot, ALU.mult, ALU.add))
                link(dve.scalar_tensor_tensor(out, turn, -c2, red, ALU.mult, ALU.add))
                link(dve.scalar_tensor_tensor(red, turn, -c3, out, ALU.mult, ALU.add))
                link(dve.tensor_scalar(turn, red, shift, 3.1415925, ALU.add, ALU.min))
                dve.tensor_scalar(out, turn, -3.1415925, None, ALU.max).then_inc(trig, 1)
                dve.wait_ge(trig, 1 if out is cosr else 2)
            dve.wait_ge(trig_act, 1)
            link(dve.scalar_tensor_tensor(red, cosr, float(DH) ** -0.5, spiral, ALU.mult, ALU.mult))
            dve.wait_ge(trig_act, 2)
            for n, scale, bias, at in (("q", red, bq, 0), ("k", sinr, bk, GROUPS)):
                dve.tensor_tensor(bias[:, :], bias_in[:, at:at + GROUPS], scale[:, S:L], ALU.mult)
                dve.tensor_tensor(w_in[n][:, :, :], w_in[n][:, :, :],
                                  scale[:, 0:S].unsqueeze(1).to_broadcast([P, NT, S]), ALU.mult).then_inc(w_ready, 1)

            def lo(part, b, g, name, out, hi_tile, bias=None, rows=slice(0, P)):
                dve.wait_ge(hi_ready, number(part, b, g, name, HI))
                src = ps_d[rows, :]
                if bias is None:
                    dve.tensor_tensor(out, src, hi_tile.bitcast(F32), ALU.subtract).then_inc(dense_done, 1)
                else:
                    dve.scalar_tensor_tensor(out, src, bias, hi_tile.bitcast(F32), ALU.add, ALU.subtract).then_inc(dense_done, 1)

            def dense(part, b, parity, g, name):
                nb, npar = (0, 0) if part == "prologue" else (b + 1, 1 - parity)
                if name in ("pq", "pk"):
                    gg = g if part == "prologue" else (g + 2) % GROUPS
                    hi_t, lo_t, bias = (q_hi, q_lo, bq) if name == "pq" else (k_hi, k_lo, bk)
                    lo(part, b, g, name, lo_t[:, :], hi_t[:, :], bias[:, gg:gg + 1])
                elif name == "tu":
                    lo(part, b, g, name, e_lo[npar][:, :], e_hi[npar][:, :])
                elif name == "tr":
                    lo(part, b, g, name, x_stk[E_DIM:P, :], x_hi[E_DIM:P, :], rows=slice(E_DIM, P))
                elif name in ("aq", "ak", "av"):
                    lo(part, b, g, name, a_lo[name[1]][:, :], a_hi[name[1]][:, :])
                elif name == "mt":
                    lo(part, b, g, name, m_parts[DH:DH + GH, :], m_parts[0:GH, :], rows=slice(0, GH))
                elif name == "mean":
                    dve.wait_ge(dense_full, number(part, b, g, name))
                    dve.tensor_tensor(cent2[:, :, :, :], emb[:, :, :].unsqueeze(2).to_broadcast([P, NT, 2, E_DIM]),
                                      ps_d[:, 0:E_DIM].unsqueeze(1).unsqueeze(1).to_broadcast([P, NT, 2, E_DIM]),
                                      ALU.subtract).then_inc(dense_done, 1)
                elif name.startswith("h0_"):
                    st = int(name[3])
                    dve.wait_ge(dense_full, number(part, b, g, name))
                    dve.bn_stats(bn1[:, st, :], ps_d[:, :]).then_inc(dense_done, 1)
                    if st == NT - 1:
                        variance(part, b, g, nb)
                elif name in WO:
                    h1_rows(part, b, g, int(name[2]))

            def variance(part, b, g, nb):
                dve.wait_ge(dense_done, number(part, b, g, "h0_3"))
                stand_alone(dve, dve_waited)
                for st in range(NT):
                    dve.bn_aggr(mv1[:, st, :], bn1[:, st, :]).then_inc(ln1, 1)
                dve.wait_ge(ln1, 10 * nb + 4)
                dve.tensor_scalar(ve1[:, :], mv1[:, :, 1], EPS, None, ALU.add).then_inc(ln1, 1)

            def newton(nb):
                dve.wait_ge(rsq, 2 * (nb + 1))
                dve.tensor_tensor(t1[:, :], y1[:, :], y1[:, :], ALU.mult).then_inc(ln1, 1)
                dve.wait_ge(ln1, 10 * nb + 6)
                dve.tensor_tensor(ln1v[:, :], t1[:, :], ve1[:, :], ALU.mult).then_inc(ln1, 1)
                dve.wait_ge(ln1, 10 * nb + 7)
                dve.tensor_scalar(t1[:, :], ln1v[:, :], -0.5, 1.5, ALU.mult, ALU.add).then_inc(ln1, 1)
                dve.wait_ge(ln1, 10 * nb + 8)
                dve.scalar_tensor_tensor(r8[:, :], y1[:, :], 0.125, t1[:, :], ALU.mult, ALU.mult).then_inc(ln1, 1)
                dve.wait_ge(ln1, 10 * nb + 9)
                dve.tensor_tensor(emb2[:, :, :, :], emb[:, :, :].unsqueeze(2).to_broadcast([P, NT, 2, E_DIM]),
                                  r8[:, :].unsqueeze(2).unsqueeze(2).to_broadcast([P, NT, 2, E_DIM]),
                                  ALU.mult).then_inc(ln1, 1)

            def row_max(k, g, u):
                dve.wait_ge(s1_full, UNITS * k + u + 1)
                j, st = u // NT, u % NT
                dve.tensor_reduce(negmax[:, g % 2, st, j:j + 1], ps_s1[:, u % 2, :], AX_X, ALU.max, negate=True).then_inc(max_done, 1)

            def scale_o(k):
                dve.wait_ge(rden, k + 1)
                dve.wait_ge(raw_copied, k + 1)
                dve.tensor_tensor(o_sb[:, :], o_raw[:, :], o_sb[:, :], ALU.mult).then_inc(o_scaled, 1)

            def o_lo_part(k, gk):
                dve.wait_ge(ohi_done, k + 1)
                dve.scalar_tensor_tensor(o_lo[:, gk, :], o_sb[:, :], bv[:, gk:gk + 1], o_hi[:, gk, :].bitcast(F32),
                                         ALU.add, ALU.subtract).then_inc(olo_done, 1)

            def h1_rows(part, b, g, st):
                pb_ = B - 1 if part == "epilogue" else b - 1
                if st:
                    centered_max(pb_, st - 1)
                dve.wait_ge(dense_full, number(part, b, g, f"wo{st}"))
                dve.tensor_tensor(h1[:, st % 2, :], ps_d[:, :], bo[:, :], ALU.add).then_inc(dense_done, 1)
                dve.wait_ge(dense_done, number(part, b, g, f"wo{st}"))
                dve.bn_stats(bn2[:, :], h1[:, st % 2, :]).then_inc(ln2, 1)
                dve.wait_ge(ln2, 17 * pb_ + 4 * st + 1)
                stand_alone(dve, dve_waited)
                dve.bn_aggr(mv2[:, st, 0:2], bn2[:, :]).then_inc(ln2, 1)
                dve.wait_ge(ln2, 17 * pb_ + 4 * st + 2)
                dve.tensor_scalar(negm[:, st:st + 1], mv2[:, st, 0:1], -1.0, None, ALU.mult).then_inc(ln2, 1)

            def centered_max(pb_, st):
                dve.wait_ge(xc_ready, NT * pb_ + st + 1)
                dve.tensor_reduce(mv2[:, st, 2:3], xc[:, st % 2, :], AX_X, ALU.max, apply_absolute_value=True).then_inc(ln2, 1)

            def keep_stats(pb_):
                dve.wait_ge(ln2, 17 * pb_ + 16)
                dve.tensor_copy(stats[:, bass.ds(12 * pb_, 12)], mv2[:, :, :].rearrange("p t c -> p (t c)")).then_inc(ln2, 1)

            for g, _, name in PROLOGUE:
                if name == "aq":
                    dve.wait_ge(wo_loaded, 16)
                    dve.wait_ge(wo_ready, 1)
                    dve.tensor_tensor(wo_lo[:, :, :], wo_stage, wo_hi[:, :, :].bitcast(F32), ALU.subtract).then_inc(wo_ready, 1)
                if name == "tr":
                    newton(0)
                if name == "av":
                    for u in range(UNITS):
                        row_max(0, 0, u)
                dense("prologue", 0, 0, g, name)
            for u in range(AHEAD):
                row_max(1, 1, u)

            def batch(part, b, parity):
                for g in range(GROUPS):
                    k = GROUPS * b + g
                    start = part == "first" and g == 0
                    for i in range(UNITS):
                        u = i + AHEAD
                        if u < UNITS and not (part == "last" and g + 1 >= GROUPS):
                            row_max(k + 1, (g + 1) % GROUPS, u)
                        if u >= UNITS and not (part == "last" and g + 2 >= GROUPS):
                            row_max(k + 2, (g + 2) % GROUPS, u - UNITS)
                        for name in items_at(part, g, i):
                            dense(part, b, parity, g, name)
                        if i == 8 and not start:
                            scale_o(k - 1)
                        if i == 10 and not start:
                            o_lo_part(k - 1, g - 1 if g else GROUPS - 1)
                        if g == 1 and i == 11 and part != "last":
                            newton(b + 1)
                        if g == 1 and i == 3 and part != "first":
                            centered_max(b - 1, NT - 1)
                            keep_stats(b - 1)

            for_batches(dve, batch)
            scale_o(STEPS - 1)
            o_lo_part(STEPS - 1, GROUPS - 1)
            for st in range(NT):
                h1_rows("epilogue", B - 1, 0, st)
            centered_max(B - 1, NT - 1)
            keep_stats(B - 1)

        @block.gpsimd
        def _(pool):
            pool.memset(ident[:, :], 0.0).then_inc(pool_const, 1)
            pool.wait_ge(pool_const, 1)
            pool.affine_select(out=ident[:, :], in_=ident[:, :], compare_op=ALU.not_equal, fill=1.0, base=0,
                               pattern=[[-1, P]], channel_multiplier=1).then_inc(pool_const, 1)

            def gather(nb, first):
                pool.wait_ge(ids_loaded, 16 * (nb + 1))
                if not first:
                    pool.wait_ge(ln1, 10 * nb)
                    pool.wait_ge(emb2_ready, nb)
                    stand_alone(pool, pool_waited)
                for tt in range(NT):
                    pool.indirect_dma_start(emb[:, tt, :], None, d["table"],
                                            bass.IndirectOffsetOnAxis(ap=ids[:, tt:tt + 1].bitcast(U32), axis=0)).then_inc(gathered, 16)

            def double(part, b, nb, first):
                pool.wait_ge(gathered, 16 * NT * (nb + 1))
                if not first:
                    if part == "first":
                        pool.wait_ge(dense_full, number("prologue", 0, 0, "tr"))
                    else:
                        pool.wait_ge(dense_full, number("mid", b - 1, 1, "tr"))
                stand_alone(pool, pool_waited)
                pool.tensor_scalar(emb2[:, :, :, :], emb[:, :, :].unsqueeze(2).to_broadcast([P, NT, 2, E_DIM]),
                                   1.0, 0.0, ALU.mult, ALU.add).then_inc(emb2_ready, 1)

            def stack_e(part, b, g, nb, par):
                pool.wait_ge(hi_ready, number(part, b, g, "tu", HI))
                stand_alone(pool, pool_waited)
                pool.tensor_scalar(e_stk8[par][0:E_DIM, :], e_hi[par][0:E_DIM, :].bitcast(F32), 0.125, 0.0,
                                   ALU.mult, ALU.add).then_inc(stk8_ready, 1)
                pool.wait_ge(dense_done, number(part, b, g, "tu"))
                stand_alone(pool, pool_waited)
                pool.tensor_scalar(e_stk8[par][E_DIM:P, :], e_lo[par][E_DIM:P, :].bitcast(F32), 0.125, 0.0,
                                   ALU.mult, ALU.add).then_inc(stk8_ready, 1)

            def stack_x(part, b, g, nb):
                pool.wait_ge(hi_ready, number(part, b, g, "tr", HI))
                stand_alone(pool, pool_waited)
                pool.tensor_scalar(x_stk[0:E_DIM, :], x_hi[0:E_DIM, :].bitcast(F32), 1.0, 0.0,
                                   ALU.mult, ALU.add).then_inc(xtop_ready, 1)

            def add(k, a):
                pool.wait_ge(pv_done, NT * k + a + 2)
                if a:
                    pool.wait_ge(added, 3 * k + a)
                pool.tensor_tensor(probs[:, a + 1, :, :], probs[:, a, :, :], probs[:, a + 1, :, :], ALU.add).then_inc(added, 1)

            gather(0, True)
            double("prologue", 0, 0, True)
            stack_e("prologue", 0, 0, 0, 0)
            stack_x("prologue", 0, 0, 0)

            def batch(part, b, parity):
                for g in range(GROUPS):
                    k = GROUPS * b + g
                    if not (part == "first" and g == 0):
                        add(k - 1, 2)
                    if g == 0 and part != "last":
                        gather(b + 1, False)
                    if g == 1 and part != "last":
                        double(part, b, b + 1, False)
                        stack_e(part, b, g, b + 1, 1 - parity)
                    add(k, 0)
                    if g == 1 and part != "last":
                        stack_x(part, b, g, b + 1)
                    add(k, 1)

            for_batches(pool, batch)
            add(STEPS - 1, 2)


def linear_block(nc, d, xc_dram, stats, out):
    with ExitStack() as ctx:
        def sb(name, shape, dt=F32):
            return ctx.enter_context(nc.sbuf_tensor("lin_" + name, shape, dt))

        def pb(name, shape, dt=F32):
            return ctx.enter_context(nc.psum_tensor("lin_" + name, shape, dt))

        def sem(name):
            return ctx.enter_context(nc.semaphore("lin_" + name))

        TILES = B * NT
        BUFS = 4
        wf = sb("wf", [P, NT, S])
        wf_y, wf_c = sb("wf_y", [P, NT, S]), sb("wf_c", [P, NT, S])
        wf_q = sb("wf_q", [P, NT, S], BF16)
        fb = sb("fb", [P, S])
        fb_r = sb("fb_r", [P, S])
        fb_h = sb("fb_h", [P, S], BF16)
        fb3 = sb("fb3", [3 * DH, S], BF16)
        sel3 = sb("sel3", [3 * DH, P], BF16)
        identb = sb("identb", [P, P], BF16)
        row = {n: sb(n, [P, TILES]) for n in ("f_ve", "f_ln", "f_y", "f_t", "f_t2", "f_r")}
        a_mean = sb("a_mean", [P, B, 2, NT])
        cur = sb("cur", [P, BUFS, 2, NT])
        am, amr = sb("am", [P, 2]), sb("amr", [P, 2])
        sc = sb("sc", [P, 8])
        x = [sb(f"x{i}", [P, NT, S]) for i in range(BUFS)]
        y = [sb(f"y{i}", [P, NT, S]) for i in range(2)]
        c = [sb(f"c{i}", [P, NT, S]) for i in range(2)]
        q = [sb(f"q{i}", [P, NT, S], BF16) for i in range(2)]
        qt = [sb(f"qt{i}", [P, NT, S], BF16) for i in range(2)]
        o = [sb(f"o{i}", [P, NT, S]) for i in range(2)]
        ps_t = pb("ps_t", [P, NT, 2 * S], BF16)
        ps_f = pb("ps_f", [P, NT, S])

        w_loaded, fb_loaded = sem("w_loaded"), sem("fb_loaded")
        x_loaded = [sem(f"x_loaded{i}") for i in range(BUFS)]
        f_const = sem("f_const")
        f_dve, f_act, f_pool = sem("f_dve"), sem("f_act"), sem("f_pool")
        wq_done = sem("wq_done")
        set_up = sem("set_up")
        cur_ready = sem("cur_ready")
        y_ready = sem("y_ready")
        r_ready = sem("r_ready")
        masked = sem("masked")
        c_ready = sem("c_ready")
        rounded = sem("rounded")
        q_ready = sem("q_ready")
        turned = sem("turned")
        qt_ready = sem("qt_ready")
        f_full = sem("f_full")
        o_ready = sem("o_ready")
        stored = [sem(f"stored{i}") for i in range(2)]

        def iterations(eng, body):
            for it in (0, 1):
                body(it, it)
            with eng.Fori(0, (B - 4) // 4) as four:
                i = eng.snap(four * 4 + 2)
                for m in range(4):
                    body(i + m, 2 + m, True)
            for it in range(B - 2, B + 2):
                body(it, it)

        def stages(it, m, mid):
            return [(it - n if mid or 0 <= it - n < B else None) for n in range(3)]

        block = ctx.enter_context(nc.Block())

        @block.sync
        def _(sp):
            sp.dma_start(wf[:, :, :], d["wf"].rearrange("(t p) n -> p t n", p=P)).then_inc(w_loaded, 16)
            sp.dma_start(fb[:, :], d["fb_row"].partition_broadcast(P).rearrange("p a n -> p (a n)")).then_inc(fb_loaded, 16)

            def load(b, i, n):
                sp.dma_start(x[i][:, :, :], xc_dram[b].rearrange("t p n -> p t n")).then_inc(x_loaded[i], 16)

            load(0, 0, 0)
            load(1, 1, 0)

            def body(it, m, mid=False):
                a, _, cc = stages(it, m, mid)
                if mid or it + 2 < B:
                    if mid or it + 2 >= BUFS:
                        sp.wait_ge(o_ready, NT * (it - 1))
                    load(it + 2, (m + 2) % BUFS, 0)
                if cc is not None:
                    sp.wait_ge(o_ready, NT * (cc + 1))
                    sp.dma_start(out[cc].rearrange("(t p) n -> p t n", p=P), o[m % 2][:, :, :]).then_inc(stored[m % 2], 16)

            iterations(sp, body)
            for i in range(2):
                sp.wait_ge(stored[i], 16 * B // 2)

        @block.scalar
        def _(act):
            act.wait_ge(f_dve, 1)
            act.activation(row["f_ln"][:, :], row["f_ve"][:, :], ACT.Ln).then_inc(f_act, 1)
            act.wait_ge(f_act, 1)
            act.activation(row["f_y"][:, :], row["f_ln"][:, :], ACT.Exp, scale=-0.5).then_inc(f_act, 1)

            def body(it, m, mid=False):
                a, bb, _ = stages(it, m, mid)
                if a is not None:
                    act.wait_ge(x_loaded[m % BUFS], 16 * ((it - m % BUFS) // BUFS + 1) if not mid else x_count(it, m))
                    act.wait_ge(cur_ready, it + 1)
                    if mid or it >= 2:
                        act.wait_ge(q_ready, it - 1)
                    for st in range(NT):
                        act.activation(y[m % 2][:, st, :], x[m % BUFS][:, st, :], ACT.Identity,
                                       scale=cur[:, m % BUFS, 0, st:st + 1]).then_inc(y_ready, 1)
                if bb is not None:
                    for st in range(NT):
                        act.wait_ge(turned, NT * bb + st + 1)
                        if st == 0 and (mid or bb >= 2):
                            act.wait_ge(f_full, NT * (bb - 1))
                        act.copy(qt[(m + 1) % 2][:, st, :], ps_t[:, st, 0:S]).then_inc(qt_ready, 1)
                if a is not None:
                    act.wait_ge(y_ready, NT * (it + 1))
                    for st in range(NT):
                        act.activation(x[m % BUFS][:, st, :], x[m % BUFS][:, st, :], ACT.Identity,
                                       bias=cur[:, m % BUFS, 1, st:st + 1]).then_inc(r_ready, 1)

            def x_count(it, m):
                return (it - m % BUFS) * (16 // BUFS) + 16

            iterations(act, body)

        @block.vector
        def _(dve):
            steps = [0]

            def link(ins):
                steps[0] += 1
                ins.then_inc(f_dve, 1)
                dve.wait_ge(f_dve, steps[0])

            st3 = stats[:, :].rearrange("p (t c) -> p t c", c=3)
            link(dve.tensor_scalar(row["f_ve"][:, :], st3[:, :, 1], EPS, None, ALU.add))
            dve.memset(identb[:, :], 0.0).then_inc(f_const, 1)
            link(dve.memset(sel3[:, :], 0.0))
            for i in range(3):
                link(dve.memset(sel3[i * DH:i * DH + 1, :], 1.0))
            dve.wait_ge(f_act, 2)
            link(dve.tensor_tensor(row["f_t"][:, :], row["f_y"][:, :], row["f_y"][:, :], ALU.mult))
            link(dve.tensor_tensor(row["f_t2"][:, :], row["f_t"][:, :], row["f_ve"][:, :], ALU.mult))
            link(dve.tensor_scalar(row["f_t"][:, :], row["f_t2"][:, :], -0.5, 1.5, ALU.mult, ALU.add))
            link(dve.tensor_tensor(row["f_r"][:, :], row["f_y"][:, :], row["f_t"][:, :], ALU.mult))
            link(dve.tensor_tensor(row["f_t"][:, :], row["f_r"][:, :], st3[:, :, 2], ALU.mult))
            link(dve.tensor_reduce(am[:, 0:1], row["f_t"][:, :], AX_X, ALU.max))
            dve.wait_ge(w_loaded, 16)
            link(dve.tensor_reduce(am[:, 1:2], wf[:, :, :].rearrange("p t n -> p (t n)"), AX_X, ALU.max, apply_absolute_value=True))
            dve.tensor_copy(amr[:, :], am[:, :]).then_inc(set_up, 1)
            dve.wait_ge(f_pool, 3)
            link(dve.tensor_scalar(sc[:, 0:1], amr[:, 0:1], 1.0 / FP8_RANGE, None, ALU.mult))
            link(dve.tensor_tensor(sc[:, 6:7], amr[:, 0:1], amr[:, 1:2], ALU.max))
            link(dve.tensor_scalar(sc[:, 1:2], sc[:, 6:7], 1.0 / FP8_RANGE, None, ALU.mult))
            link(dve.reciprocal(sc[:, 2:4], sc[:, 0:2]))
            link(dve.tensor_tensor(sc[:, 4:5], sc[:, 0:1], sc[:, 1:2], ALU.mult))
            link(dve.reciprocal(sc[:, 5:6], sc[:, 4:5]))
            link(dve.tensor_scalar(a_mean[:, :, 0, :], row["f_r"][:, :].rearrange("p (b t) -> p b t", t=NT), sc[:, 2:3], None, ALU.mult))
            link(dve.tensor_copy(a_mean[:, :, 1, :], st3[:, :, 0].rearrange("p (b t) -> p b t", t=NT)))

            def mask(out, src):
                return dve.tensor_scalar(out.bitcast(U32), src.bitcast(U32), 0x7F800000, None, ALU.bitwise_and)

            def shifter(out, src):
                return dve.tensor_scalar(out, src, 2.0 ** -6, 1.5 * 2.0 ** 20, ALU.max, ALU.mult)

            link(dve.tensor_scalar(wf_y[:, :, :], wf[:, :, :], sc[:, 3:4], None, ALU.mult))
            link(mask(wf_c[:, :, :], wf_y[:, :, :]))
            link(shifter(wf_c[:, :, :], wf_c[:, :, :]))
            link(dve.tensor_tensor(wf_y[:, :, :], wf_y[:, :, :], wf_c[:, :, :], ALU.add))
            link(dve.tensor_tensor(wf_q[:, :, :], wf_y[:, :, :], wf_c[:, :, :], ALU.subtract))
            dve.wait_ge(fb_loaded, 16)
            link(dve.tensor_scalar(fb_r[:, :], fb[:, :], sc[:, 5:6], None, ALU.mult))
            link(dve.tensor_copy(fb_h[:, :], fb_r[:, :]))
            link(dve.tensor_copy(fb3[0:DH, :], fb_r[0:DH, :]))
            link(dve.tensor_tensor(fb[:, :], fb_r[:, :], fb_h[:, :], ALU.subtract))
            link(dve.tensor_copy(fb3[DH:2 * DH, :], fb[DH:2 * DH, :]))
            link(dve.tensor_copy(fb_h[:, :], fb[:, :]))
            link(dve.tensor_tensor(fb_r[:, :], fb[:, :], fb_h[:, :], ALU.subtract))
            dve.tensor_copy(fb3[2 * DH:3 * DH, :], fb_r[2 * DH:3 * DH, :]).then_inc(wq_done, 1)

            def body(it, m, mid=False):
                a, bb, cc = stages(it, m, mid)
                if a is not None:
                    dve.tensor_copy(cur[:, m % BUFS, :, :].rearrange("p c t -> p (c t)"),
                                    a_mean[:, :, :, :].rearrange("p b c t -> p (b c t)")[:, bass.ds(2 * NT * it, 2 * NT)]).then_inc(cur_ready, 1)
                if cc is not None:
                    for st in range(NT):
                        dve.wait_ge(f_full, NT * cc + st + 1)
                        if st == 0:
                            dve.wait_ge(r_ready, NT * (cc + 1))
                            if mid or cc >= 2:
                                dve.wait_ge(stored[m % 2], 8 * (cc - m % 2))
                        dve.scalar_tensor_tensor(o[m % 2][:, st, :], ps_f[:, st, :], sc[:, 4:5], x[(m - 2) % BUFS][:, st, :],
                                                 ALU.mult, ALU.add).then_inc(o_ready, 1)
                if bb is not None:
                    dve.wait_ge(rounded, bb + 1)
                    if mid or bb >= 2:
                        dve.wait_ge(turned, NT * (bb - 1))
                    dve.tensor_tensor(q[(m + 1) % 2][:, :, :], y[(m + 1) % 2][:, :, :], c[(m + 1) % 2][:, :, :],
                                      ALU.subtract).then_inc(q_ready, 1)
                if a is not None:
                    dve.wait_ge(y_ready, NT * (it + 1))
                    if mid or it >= 2:
                        dve.wait_ge(q_ready, it - 1)
                    mask(c[m % 2][:, :, :], y[m % 2][:, :, :]).then_inc(masked, 1)
                    dve.wait_ge(masked, it + 1)
                    shifter(c[m % 2][:, :, :], c[m % 2][:, :, :]).then_inc(c_ready, 1)

            iterations(dve, body)

        @block.gpsimd
        def _(pool):
            pool.wait_ge(f_const, 1)
            pool.affine_select(out=identb[:, :], in_=identb[:, :], compare_op=ALU.not_equal, fill=1.0, base=0,
                               pattern=[[-1, P]], channel_multiplier=1).then_inc(f_pool, 1)
            pool.wait_ge(set_up, 1)
            pool.partition_all_reduce(amr[:, 0:1], am[:, 0:1], P, bass.bass_isa.ReduceOp.max).then_inc(f_pool, 1)
            pool.partition_all_reduce(amr[:, 1:2], am[:, 1:2], P, bass.bass_isa.ReduceOp.max).then_inc(f_pool, 1)

            def body(it, m, mid=False):
                a, _, _ = stages(it, m, mid)
                if a is not None:
                    pool.wait_ge(c_ready, it + 1)
                    pool.tensor_tensor(y[m % 2][:, :, :], y[m % 2][:, :, :], c[m % 2][:, :, :], ALU.add).then_inc(rounded, 1)

            iterations(pool, body)

        @block.tensor
        def _(pe):
            pe.wait_ge(f_pool, 1)
            pe.wait_ge(wq_done, 1)

            def body(it, m, mid=False):
                _, bb, _ = stages(it, m, mid)
                if bb is None:
                    return
                pe.wait_ge(q_ready, bb + 1)
                for st in range(NT):
                    if mid or bb >= 1:
                        pe.wait_ge(qt_ready, NT * (bb - 1) + st + 1)
                    for ib in range(NT):
                        last = pe.transpose(ps_t[:, st, ib * P:(ib + 1) * P], q[(m + 1) % 2][:, st, ib * P:(ib + 1) * P], identb[:, :])
                    last.then_inc(turned, 1)
                for st in range(NT):
                    pe.wait_ge(qt_ready, NT * bb + st + 1)
                    if mid or bb >= 1:
                        pe.wait_ge(o_ready, NT * (bb - 1) + st + 1)
                    pe.matmul(ps_f[:, st, :], sel3[:, :], fb3[:, :], start=True, stop=False)
                    for ib in range(NT):
                        last = pe.matmul(ps_f[:, st, :], qt[(m + 1) % 2][:, st, ib * P:(ib + 1) * P], wf_q[:, ib, :],
                                         start=False, stop=(ib == NT - 1))
                    last.then_inc(f_full, 1)

            iterations(pe, body)


def tower(nc, d, out):
    with ExitStack() as ctx:
        stats = ctx.enter_context(nc.sbuf_tensor("stats", [P, B * NT * 3], F32))
        xc_dram = nc.dram_tensor("xc_dram", (B, NT, P, S), F32, kind="Internal").ap()
        attention_block(nc, d, xc_dram, stats)
        linear_block(nc, d, xc_dram, stats, out)


def kernel(**inputs):
    import numpy as np
    from concourse import bacc
    from concourse.bass_utils import run_bass_kernel_spmd

    nc = bacc.Bacc("TRN2", target_bir_lowering=False, num_devices=1, dynamic_dma_scratch_size=4096)
    a = {n: np.asarray(v) for n, v in inputs.items()}

    def by_dim(v):
        return v.reshape((GROUPS, GH, DH) + v.shape[1:]).swapaxes(1, 2).reshape(v.shape)

    def cols(v):
        return v.reshape(GROUPS, P).T

    rot = by_dim(a["L0_attn_helix_rotation"])
    spiral = by_dim(np.repeat(a["L0_attn_spiral_weight"], DH))
    arrays = {
        "ids": a["x"].reshape(B, NT, P).swapaxes(1, 2),
        "table": a["L0_tok_weight"],
        "wq": by_dim(a["L0_attn_Wq"]).T, "wk": by_dim(a["L0_attn_Wk"]).T, "wv": a["L0_attn_Wv"].T,
        "wo": a["L0_attn_Wo"].T, "wf": a["L0_ffn_weight"].T,
        "bq_col": cols(by_dim(a["L0_attn_bq"])), "bk_col": cols(by_dim(a["L0_attn_bk"])), "bv_col": cols(a["L0_attn_bv"]),
        "bo_row": a["L0_attn_bo"][None], "fb_row": a["L0_ffn_bias"][None],
        "rot_row": rot[None], "rot_col": cols(rot), "spiral_row": spiral[None], "spiral_col": cols(spiral),
    }
    arrays = {f"in_{n}": np.ascontiguousarray(v) for n, v in arrays.items()}
    d = {n[3:]: nc.dram_tensor(n, v.shape, mybir.dt.from_np(v.dtype), kind="ExternalInput").ap() for n, v in arrays.items()}
    out = nc.dram_tensor("out", (B, S, S), F32, kind="ExternalOutput").ap()
    tower(nc, d, out)
    r = run_bass_kernel_spmd(nc, [arrays], core_ids=[0])
    return r.results[0]["out"]
```

```python
from contextlib import ExitStack

import concourse.bass as bass
from concourse import mybir

ALU = mybir.AluOpType
ACT = mybir.ActivationFunctionType
AX_X = mybir.AxisListType.X
F32 = mybir.dt.float32
F32R = mybir.dt.float32r
BF16 = mybir.dt.bfloat16
I32 = mybir.dt.int32
U32 = mybir.dt.uint32

P = 128
B = 16
S = 512
E_DIM = 64
HEADS = 16
DH = S // HEADS
GH = 4
GROUPS = HEADS // GH
NT = S // P
STEPS = B * GROUPS
UNITS = GH * NT
DENSE_BANKS = 3
S2_BANKS = 2
AHEAD = 5
QK_ROWS = 3 * DH
QKM_ROWS = QK_ROWS + 2
EPS = 1e-5
FP8_RANGE = 448.0 * 0.8
MAGIC = 1.5 * 2.0 ** 23

DEN = 8
MID = [(0, 0, "v0"), (0, 1, "pq"), (0, 3, "pk"), (0, 4, "v1"), (0, 6, "v2"), (0, DEN, "den"), (0, 10, "v3"),
       (0, 12, "wo0"), (0, 13, "mt"), (0, 15, "wo1"),
       (1, 1, "pq"), (1, 2, "wo2"), (1, 4, "pk"), (1, 5, "wo3"), (1, 6, "mean"), (1, 7, "tu"), (1, DEN, "den"),
       (1, 9, "h0_0"), (1, 10, "h0_1"), (1, 11, "h0_2"), (1, 12, "mt"), (1, 13, "h0_3"), (1, 14, "aq"),
       (2, 0, "ak"), (2, 3, "tr"), (2, 5, "pq"), (2, 7, "pk"), (2, DEN, "den"), (2, 12, "mt"),
       (3, 1, "pq"), (3, 3, "pk"), (3, DEN, "den"), (3, 10, "av"), (3, 12, "mt")]
CENTER_AT = ((0, 14), (1, 1), (1, 4), (1, 7))
PREPARE = ("mean", "tu", "h0_0", "h0_1", "h0_2", "h0_3", "aq", "tr", "ak", "av")
WO = ("wo0", "wo1", "wo2", "wo3")
FIRST = [x for x in MID if x[2] not in WO and x[::2] != (0, "den")]
LAST = [x for x in MID if x[2] not in PREPARE and not (x[0] >= 2 and x[2] in ("pq", "pk")) and x[::2] != (3, "mt")]
PROLOGUE = [(0, 0, n) for n in ("mean", "tu", "h0_0", "h0_1", "h0_2", "h0_3", "aq", "tr", "ak")] + [
    (0, 0, "pq"), (0, 0, "pk"), (1, 0, "pq"), (1, 0, "pk"), (0, 0, "av"), (0, 0, "mt")]
EPILOGUE = [(0, 0, "den")] + [(0, 0, n) for n in WO]
ITEMS = {"prologue": PROLOGUE, "first": FIRST, "mid": MID, "last": LAST, "epilogue": EPILOGUE}
HI = ("pq", "pk", "mt", "tu", "tr", "aq", "ak", "av")


def bank_of(part, g, name):
    return [x[::2] for x in ITEMS[part]].index((g, name)) % DENSE_BANKS


def count(part, b, g, name, counts):
    def size(p, upto=None):
        return sum(1 for gg, _, n in ITEMS[p][:upto] if counts(p, gg, n))

    here = size(part, [x[::2] for x in ITEMS[part]].index((g, name)) + 1)
    if part == "prologue":
        return here
    if part == "first":
        return size("prologue") + here
    base = size("prologue") + size("first")
    if part == "mid":
        return base + (b - 1) * size("mid") + here
    base += (B - 2) * size("mid")
    return base + here if part == "last" else base + size("last") + here


def number(part, b, g, name):
    return count(part, b, g, name, lambda *x: True)


def hi_number(part, b, g, name):
    return count(part, b, g, name, lambda p, gg, n: n in HI)


def bank_number(part, b, g, name):
    bank = bank_of(part, g, name)
    return count(part, b, g, name, lambda p, gg, n: bank_of(p, gg, n) == bank)


def s2_bank(i):
    return 1 if i == UNITS - 1 and UNITS % S2_BANKS == 1 else i % S2_BANKS


def s2_back(i):
    return next(n for n in range(1, UNITS + 1) if s2_bank((i - n) % UNITS) == s2_bank(i))


def items_at(part, g, slot):
    return [n for gg, ss, n in ITEMS[part] if gg == g and ss == slot]


def for_batches(eng, body):
    body("first", 0, 0)
    with eng.Fori(0, (B - 2) // 2) as pair:
        b = eng.snap(pair * 2 + 1)
        body("mid", b, 1)
        body("mid", b + 1, 0)
    body("last", B - 1, 1)


def stand_alone(eng, sem):
    eng.sem_inc(sem, 1)


def attention_block(nc, d, xc_dram, stats):
    with ExitStack() as ctx:
        def sb(name, shape, dt=F32):
            return ctx.enter_context(nc.sbuf_tensor(name, shape, dt))

        def pb(name, shape):
            return ctx.enter_context(nc.psum_tensor(name, shape, F32))

        def sem(name):
            return ctx.enter_context(nc.semaphore(name))

        w_in = {n: sb(f"w_{n}", [P, NT, S]) for n in "qkv"}
        wo_hi, wo_lo = sb("wo_hi", [P, NT, S], F32R), sb("wo_lo", [P, NT, S], F32R)
        bq, bk, bv = sb("bq", [P, GROUPS]), sb("bk", [P, GROUPS]), sb("bv", [P, GROUPS])
        bo = sb("bo", [P, S])
        ones_mean = sb("ones_mean", [P, P])
        ones_den = sb("ones_den", [P, DH])
        ident = sb("ident", [P, P])
        q_stack = [sb(f"q_stack{g}", [P, GH, S], F32R) for g in range(GROUPS)]
        k_stack = [sb(f"k_stack{g}", [P, GH, S], F32R) for g in range(GROUPS)]
        q_hi, q_lo = sb("q_hi", [P, S], F32R), sb("q_lo", [P, S], F32R)
        k_hi, k_lo = sb("k_hi", [P, S], F32R), sb("k_lo", [P, S], F32R)
        v_sb = sb("v_sb", [P, NT, S])
        probs = sb("probs", [P, NT, GH, S])
        o_raw, o_sb = sb("o_raw", [P, S]), sb("o_sb", [P, S])
        o_hi, o_lo = sb("o_hi", [P, GROUPS, S], F32R), sb("o_lo", [P, GROUPS, S], F32R)
        h1 = sb("h1", [P, 2, S])
        xc = sb("xc", [P, 2, S])
        negmax = sb("negmax", [P, 2, NT, GH])
        m_parts = sb("m_parts", [DH + GH, S], F32R)
        ids = sb("ids", [P, NT], I32)
        emb = sb("emb", [P, NT, E_DIM])
        emb2 = sb("emb2", [P, NT, 2, E_DIM])
        cent2 = sb("cent2", [P, NT, 2, E_DIM])
        e_hi = [sb(f"e_hi{i}", [P, S], F32R) for i in range(2)]
        e_lo = [sb(f"e_lo{i}", [P, S], F32R) for i in range(2)]
        e_stk8 = [sb(f"e_stk8_{i}", [P, S], F32R) for i in range(2)]
        x_hi = sb("x_hi", [P, S], F32R)
        x_stk = sb("x_stk", [P, S], F32R)
        a_hi = {n: sb(f"a_hi_{n}", [P, S], F32R) for n in "qkv"}
        a_lo = {n: sb(f"a_lo_{n}", [P, S], F32R) for n in "qkv"}
        bn1, mv1 = sb("bn1", [P, NT, 6]), sb("mv1", [P, NT, 2])
        ve1, ln1v, y1, t1, r8 = (sb(n, [P, NT]) for n in ("ve1", "ln1v", "y1", "t1", "r8"))
        bn2, mv2, negm = sb("bn2", [P, 6]), sb("mv2", [P, NT, 3]), sb("negm", [P, NT])

        ps_s2 = pb("ps_s2", [P, S2_BANKS, S])
        ps_s1 = pb("ps_s1", [P, 2, S])
        ps_dense = [pb(f"ps_d{i}", [P, S]) for i in range(DENSE_BANKS)]
        ps_o = pb("ps_o", [P, S])

        loaded = sem("loaded")
        wo_loaded = sem("wo_loaded")
        consts = sem("consts")
        pool_const = sem("pool_const")
        trig = sem("trig")
        trig_act = sem("trig_act")
        trig_dve = sem("trig_dve")
        w_ready = sem("w_ready")
        wo_ready = sem("wo_ready")
        ids_loaded = sem("ids_loaded")
        gathered = sem("gathered")
        emb2_ready = sem("emb2_ready")
        stk8_ready = sem("stk8_ready")
        xtop_ready = sem("xtop_ready")
        ln1 = sem("ln1")
        rsq = sem("rsq")
        dense_full = sem("dense_full")
        dense_done = [sem(f"dense_done{i}") for i in range(DENSE_BANKS)]
        hi_ready = sem("hi_ready")
        stack_loaded = sem("stack_loaded")
        m_loaded = sem("m_loaded")
        s1_full = sem("s1_full")
        max_done = sem("max_done")
        s2_full = sem("s2_full")
        exp_done = sem("exp_done")
        pv_done = sem("pv_done")
        added = sem("added")
        raw_copied = sem("raw_copied")
        rden = sem("rden")
        o_scaled = sem("o_scaled")
        ohi_done = sem("ohi_done")
        olo_done = sem("olo_done")
        ln2 = sem("ln2")
        xc_ready = sem("xc_ready")
        xc_stored = [sem(f"xc_stored{i}") for i in range(2)]

        dve_waited, pool_waited = sem("dve_waited"), sem("pool_waited")

        block = ctx.enter_context(nc.Block())

        def wait_done(eng, part, b, g, name):
            eng.wait_ge(dense_done[bank_of(part, g, name)], bank_number(part, b, g, name))

        wo_stage = probs[:, 0, :, :]
        L = S + GROUPS
        flat = probs[:, 1:4, :, :].rearrange("p a h n -> p (a h n)")

        def region(i):
            return flat[:, i * L:(i + 1) * L]

        rot, spiral, cosr, sinr, turn, red = (region(i) for i in range(6))
        bias_in = region(6)
        LOADS = 11

        @block.sync
        def _(sp):
            for i in range(2):
                sp.sem_inc(xc_stored[i], 16)
            sp.dma_start(ids[:, :], d["ids"][0]).then_inc(ids_loaded, 16)
            sp.dma_start(rot[:, 0:S], d["rot_row"].partition_broadcast(P).rearrange("p a n -> p (a n)")).then_inc(loaded, 16)
            sp.dma_start(rot[:, S:L], d["rot_col"]).then_inc(loaded, 16)
            sp.dma_start(spiral[:, 0:S], d["spiral_row"].partition_broadcast(P).rearrange("p a n -> p (a n)")).then_inc(loaded, 16)
            sp.dma_start(spiral[:, S:L], d["spiral_col"]).then_inc(loaded, 16)
            sp.dma_start(bias_in[:, 0:GROUPS], d["bq_col"]).then_inc(loaded, 16)
            sp.dma_start(bias_in[:, GROUPS:2 * GROUPS], d["bk_col"]).then_inc(loaded, 16)
            for n in "qkv":
                sp.dma_start(w_in[n][:, :, :], d[f"w{n}"].rearrange("(t p) n -> p t n", p=P)).then_inc(loaded, 16)
            sp.dma_start(bv[:, :], d["bv_col"]).then_inc(loaded, 16)
            sp.dma_start(bo[:, :], d["bo_row"].partition_broadcast(P).rearrange("p a n -> p (a n)")).then_inc(loaded, 16)
            sp.dma_start(wo_stage, d["wo"].rearrange("(t p) n -> p t n", p=P)).then_inc(wo_loaded, 16)

            def load_ids(nb):
                sp.wait_ge(gathered, 16 * NT * nb)
                sp.dma_start(ids[:, :], d["ids"][nb]).then_inc(ids_loaded, 16)

            def stack_q(part, b, g, k, slot):
                sp.wait_ge(hi_ready, hi_number(part, b, g, "pq"))
                sp.dma_start(q_stack[slot][0:DH, :, :].bitcast(F32), q_hi[:, :].bitcast(F32)).then_inc(stack_loaded, 16)
                sp.dma_start(q_stack[slot][2 * DH:3 * DH, :, :].bitcast(F32), q_hi[:, :].bitcast(F32)).then_inc(stack_loaded, 16)
                wait_done(sp, part, b, g, "pq")
                sp.dma_start(q_stack[slot][DH:2 * DH, :, :].bitcast(F32), q_lo[:, :].bitcast(F32)).then_inc(stack_loaded, 16)

            def stack_k(part, b, g, k, slot):
                sp.wait_ge(hi_ready, hi_number(part, b, g, "pk"))
                sp.dma_start(k_stack[slot][0:DH, :, :].bitcast(F32), k_hi[:, :].bitcast(F32)).then_inc(stack_loaded, 16)
                sp.dma_start(k_stack[slot][DH:2 * DH, :, :].bitcast(F32), k_hi[:, :].bitcast(F32)).then_inc(stack_loaded, 16)
                wait_done(sp, part, b, g, "pk")
                sp.dma_start(k_stack[slot][2 * DH:3 * DH, :, :].bitcast(F32), k_lo[:, :].bitcast(F32)).then_inc(stack_loaded, 16)

            def max_rows(part, b, g, slot):
                sp.wait_ge(hi_ready, hi_number(part, b, g, "mt"))
                sp.dma_start(q_stack[slot][QK_ROWS:QK_ROWS + 1, :, :].bitcast(F32), m_parts[0:GH, :].bitcast(F32)).then_inc(m_loaded, 16)
                wait_done(sp, part, b, g, "mt")
                sp.dma_start(q_stack[slot][QK_ROWS + 1:QKM_ROWS, :, :].bitcast(F32), m_parts[DH:DH + GH, :].bitcast(F32)).then_inc(m_loaded, 16)

            def store_xc(pb_, st):
                sp.wait_ge(xc_ready, NT * pb_ + st + 1)
                sp.dma_start(xc_dram[pb_, st], xc[:, st % 2, :]).then_inc(xc_stored[st % 2], 16)

            stack_q("prologue", 0, 0, 0, 0)
            stack_k("prologue", 0, 0, 0, 0)
            stack_q("prologue", 0, 1, 1, 1)
            stack_k("prologue", 0, 1, 1, 1)
            max_rows("prologue", 0, 0, 0)

            def batch(part, b, parity):
                for g in range(GROUPS):
                    has = [n for gg, _, n in ITEMS[part] if gg == g]
                    if g == 0 and part != "last":
                        load_ids(b + 1)
                    if g == 1 and part != "first":
                        store_xc(b - 1, 1)
                    if "pq" in has:
                        stack_q(part, b, g, 4 * b + g + 2, (g + 2) % GROUPS)
                    if "pk" in has:
                        stack_k(part, b, g, 4 * b + g + 2, (g + 2) % GROUPS)
                    if g == 1 and part != "first":
                        for st in range(2, NT):
                            store_xc(b - 1, st)
                    if "mt" in has:
                        max_rows(part, b, g, (g + 1) % GROUPS)
                    if g == 0 and part != "first":
                        store_xc(b - 1, 0)

            for_batches(sp, batch)
            for st in range(NT):
                store_xc(B - 1, st)
            for i in range(2):
                sp.wait_ge(xc_stored[i], 16 + 16 * B * NT // 2)

        @block.tensor
        def _(pe):
            def open_dense(part, b, g, name):
                n = bank_number(part, b, g, name)
                if not (isinstance(n, int) and n == 1):
                    pe.wait_ge(dense_done[bank_of(part, g, name)], n - 1)
                return ps_dense[bank_of(part, g, name)]

            def mean(ps_d, nb):
                pe.wait_ge(gathered, 16 * NT * (nb + 1))
                for tt in range(NT):
                    last = pe.matmul(ps_d[:, 0:E_DIM], ones_mean[:, :], emb[:, tt, :], start=(tt == 0), stop=(tt == NT - 1))
                last.then_inc(dense_full, 1)

            def turn_e(ps_d, nb, scaled):
                if not scaled:
                    pe.wait_ge(emb2_ready, nb + 1)
                else:
                    pe.wait_ge(ln1, 10 * (nb + 1))
                for tt in range(NT):
                    last = pe.transpose(ps_d[:, tt * P:(tt + 1) * P], emb2[:, tt, :, :].rearrange("p c e -> p (c e)"), ident[:, :])
                last.then_inc(dense_full, 1)

            def h0_rows(ps_d, nb, par, st):
                if st == 0:
                    pe.wait_ge(stk8_ready, 2 * (nb + 1))
                w = e_stk8[par][:, st * P:(st + 1) * P]
                pe.matmul(ps_d[:, :], w, e_hi[par][:, :], start=True, stop=False)
                pe.matmul(ps_d[:, :], w, e_lo[par][:, :], start=False, stop=True).then_inc(dense_full, 1)

            def make_a(ps_d, n):
                for jt in range(NT):
                    last = pe.matmul(ps_d[:, :], cent2[:, jt, :, :].rearrange("p c e -> p (c e)"), w_in[n][:, jt, :],
                                     start=(jt == 0), stop=(jt == NT - 1))
                last.then_inc(dense_full, 1)

            def project(ps_d, n, nb, g):
                pe.wait_ge(xtop_ready, nb + 1)
                pe.matmul(ps_d[:, :], a_hi[n][:, g * P:(g + 1) * P], x_stk[:, :], start=True, stop=False)
                pe.matmul(ps_d[:, :], a_lo[n][:, g * P:(g + 1) * P], x_stk[:, :], start=False, stop=True).then_inc(dense_full, 1)

            def project_v(ps_d, tt):
                w = x_stk[:, tt * P:(tt + 1) * P]
                pe.matmul(ps_d[:, :], w, a_hi["v"][:, :], start=True, stop=False)
                pe.matmul(ps_d[:, :], w, a_lo["v"][:, :], start=False, stop=True).then_inc(dense_full, 1)

            def turn_max(ps_d, k, g):
                pe.wait_ge(max_done, UNITS * (k + 1))
                for st in range(NT):
                    last = pe.transpose(ps_d[0:GH, st * P:(st + 1) * P], negmax[:, g % 2, st, :], ident[:, :])
                last.then_inc(dense_full, 1)

            def denominators(ps_d, k):
                pe.wait_ge(added, 3 * (k + 1))
                for j in range(GH):
                    last = pe.matmul(ps_d[j * DH:(j + 1) * DH, :], ones_den[:, :], probs[:, NT - 1, j, :], start=True, stop=True)
                last.then_inc(dense_full, 1)

            def out_proj(ps_d, pb_, par, st):
                if st == 0:
                    pe.wait_ge(olo_done, GROUPS * (pb_ + 1))
                w = e_stk8[par][:, st * P:(st + 1) * P]
                pe.matmul(ps_d[:, :], w, e_hi[par][:, :], start=True, stop=False)
                pe.matmul(ps_d[:, :], w, e_lo[par][:, :], start=False, stop=False)
                for c in range(NT):
                    pe.matmul(ps_d[:, :], o_hi[:, c, st * P:(st + 1) * P], wo_hi[:, c, :], start=False, stop=False)
                    pe.matmul(ps_d[:, :], o_hi[:, c, st * P:(st + 1) * P], wo_lo[:, c, :], start=False, stop=False)
                    last = pe.matmul(ps_d[:, :], o_lo[:, c, st * P:(st + 1) * P], wo_hi[:, c, :], start=False, stop=(c == NT - 1))
                last.then_inc(dense_full, 1)

            def scores_st(k, g, u, first):
                if u == 0:
                    pe.wait_ge(stack_loaded, 96 * (k + 1))
                if not (first and u < 2):
                    pe.wait_ge(max_done, UNITS * k + u - 1)
                j, st = u // NT, u % NT
                pe.matmul(ps_s1[:, u % 2, :], q_stack[g][0:QK_ROWS, j, st * P:(st + 1) * P], k_stack[g][0:QK_ROWS, j, :],
                          start=True, stop=True).then_inc(s1_full, 1)

            def scores_ts(k, g, i, first):
                if i == 0:
                    pe.wait_ge(m_loaded, 32 * (k + 1))
                back = s2_back(i)
                if not (first and i < back):
                    pe.wait_ge(exp_done, UNITS * k + i - back + 1)
                tt, j = i // GH, i % GH
                pe.matmul(ps_s2[:, s2_bank(i), :], k_stack[g][0:QKM_ROWS, j, tt * P:(tt + 1) * P], q_stack[g][0:QKM_ROWS, j, :],
                          start=True, stop=True).then_inc(s2_full, 1)

            def times_v(k, g, tt, first, part=None, b=None):
                pe.wait_ge(exp_done, UNITS * k + GH * (tt + 1))
                if g == 0:
                    wait_done(pe, part, b, 0, f"v{tt}")
                if tt == 0 and not first:
                    pe.wait_ge(raw_copied, k)
                for j in range(GH):
                    h = g * GH + j
                    last = pe.matmul(ps_o[j * DH:(j + 1) * DH, :], v_sb[:, tt, h * DH:(h + 1) * DH], probs[:, tt, j, :],
                                     start=(tt == 0), stop=(tt == NT - 1), skip_group_check=True)
                last.then_inc(pv_done, 1)

            def dense(part, b, parity, g, name):
                ps_d = open_dense(part, b, g, name)
                nb, npar = (0, 0) if part == "prologue" else (b + 1, 1 - parity)
                if name == "mean":
                    mean(ps_d, nb)
                elif name == "tu":
                    turn_e(ps_d, nb, False)
                elif name == "tr":
                    turn_e(ps_d, nb, True)
                elif name.startswith("h0_"):
                    h0_rows(ps_d, nb, npar, int(name[3]))
                elif name in ("aq", "ak", "av"):
                    if name == "aq":
                        wait_done(pe, part, b, 0 if part == "prologue" else 1, "mean")
                    make_a(ps_d, name[1])
                elif name in ("pq", "pk"):
                    if (part, g) == ("prologue", 0) or (part != "prologue" and g == 2):
                        wait_done(pe, part, b, 0 if part == "prologue" else {"pq": 1, "pk": 2}[name], "a" + name[1])
                        wait_done(pe, part, b, 0 if part == "prologue" else 2, "tr")
                    if part == "prologue":
                        project(ps_d, name[1], 0, g)
                    else:
                        project(ps_d, name[1], b + (g + 2) // GROUPS, (g + 2) % GROUPS)
                elif name[0] == "v":
                    project_v(ps_d, int(name[1]))
                elif name == "mt":
                    if part == "prologue" or (part != "last" and g == GROUPS - 1):
                        wait_done(pe, part, b, 0 if part == "prologue" else 3, "av")
                    turn_max(ps_d, 0 if part == "prologue" else GROUPS * b + g + 1, 0 if part == "prologue" else (g + 1) % GROUPS)
                elif name == "den":
                    denominators(ps_d, STEPS - 1 if part == "epilogue" else GROUPS * b + g - 1)
                else:
                    out_proj(ps_d, B - 1 if part == "epilogue" else b - 1, 1 if part == "epilogue" else 1 - parity, int(name[2]))

            pe.wait_ge(consts, 3)
            pe.wait_ge(pool_const, 2)
            for g, _, name in PROLOGUE:
                if name == "aq":
                    pe.wait_ge(w_ready, 2)
                if name == "av":
                    for u in range(UNITS):
                        scores_st(0, 0, u, True)
                dense("prologue", 0, 0, g, name)
            pe.wait_ge(wo_ready, 2)
            for u in range(AHEAD):
                scores_st(1, 1, u, False)

            def batch(part, b, parity):
                for g in range(GROUPS):
                    k = GROUPS * b + g
                    for i in range(UNITS):
                        for name in items_at(part, g, i):
                            dense(part, b, parity, g, name)
                        u = i + AHEAD
                        if u < UNITS and not (part == "last" and g + 1 >= GROUPS):
                            scores_st(k + 1, (g + 1) % GROUPS, u, False)
                        if u >= UNITS and not (part == "last" and g + 2 >= GROUPS):
                            scores_st(k + 2, (g + 2) % GROUPS, u - UNITS, False)
                        scores_ts(k, g, i, part == "first" and g == 0)
                        if i == 1 and not (part == "first" and g == 0):
                            times_v(k - 1, g - 1 if g else GROUPS - 1, NT - 1, False, part, b)
                        if i in (5, 9, 13):
                            times_v(k, g, (i - 5) // 4, part == "first" and g == 0, part, b)

            for_batches(pe, batch)
            times_v(STEPS - 1, GROUPS - 1, NT - 1, False)
            for g, _, name in EPILOGUE:
                dense("epilogue", B - 1, 1, g, name)

        @block.scalar
        def _(act):
            act.wait_ge(trig, 1)
            act.activation(cosr, cosr, ACT.Sin).then_inc(trig_act, 1)
            act.wait_ge(trig, 2)
            act.activation(sinr, sinr, ACT.Sin).then_inc(trig_act, 1)
            act.preload_act_table_set("natural_log_exp_and_others")
            act.wait_ge(wo_loaded, 16)
            act.copy(wo_hi[:, :, :], wo_stage).then_inc(wo_ready, 1)

            def hi(part, b, g, name, out, bias=None):
                act.wait_ge(dense_full, number(part, b, g, name))
                src = ps_dense[bank_of(part, g, name)][0:out.shape[0], :]
                if bias is None:
                    act.copy(out, src).then_inc(hi_ready, 1)
                else:
                    act.activation(out, src, ACT.Identity, bias=bias).then_inc(hi_ready, 1)

            def dense(part, b, parity, g, name):
                nb, npar = (0, 0) if part == "prologue" else (b + 1, 1 - parity)
                if name in ("pq", "pk"):
                    gg = g if part == "prologue" else (g + 2) % GROUPS
                    kk = g if part == "prologue" else GROUPS * b + g + 2
                    if not (part == "prologue" and g == 0):
                        act.wait_ge(stack_loaded, 96 * kk)
                    out, bias = (q_hi, bq) if name == "pq" else (k_hi, bk)
                    hi(part, b, g, name, out[:, :], bias[:, gg:gg + 1])
                elif name == "tu":
                    hi(part, b, g, name, e_hi[npar][:, :])
                elif name == "tr":
                    if part != "prologue":
                        act.wait_ge(xtop_ready, nb)
                    hi(part, b, g, name, x_hi[:, :])
                elif name in ("aq", "ak", "av"):
                    hi(part, b, g, name, a_hi[name[1]][:, :])
                elif name == "mt":
                    if part != "prologue":
                        act.wait_ge(m_loaded, 32 * (GROUPS * b + g + 1))
                    hi(part, b, g, name, m_parts[0:GH, :])
                elif name[0] == "v":
                    tt = int(name[1])
                    if part != "first":
                        act.wait_ge(pv_done, NT * GROUPS * b - NT + tt + 1)
                    act.wait_ge(dense_full, number(part, b, g, name))
                    bank = bank_of(part, g, name)
                    act.copy(v_sb[:, tt, :], ps_dense[bank][:, :]).then_inc(dense_done[bank], 1)
                elif name == "den":
                    inverse_den(part, b, g)

            def inverse_den(part, b, g):
                k = STEPS - 1 if part == "epilogue" else GROUPS * b + g - 1
                if not (isinstance(k, int) and k == 0):
                    act.wait_ge(olo_done, k)
                act.wait_ge(dense_full, number(part, b, g, "den"))
                bank = bank_of(part, g, "den")
                act.activation(o_sb[:, :], ps_dense[bank][:, :], ACT.Ln).then_inc(dense_done[bank], 1)
                wait_done(act, part, b, g, "den")
                act.activation(o_sb[:, :], o_sb[:, :], ACT.Exp, scale=-1.0).then_inc(rden, 1)

            def rsqrt(nb):
                act.wait_ge(ln1, 10 * nb + 5)
                act.activation(ln1v[:, :], ve1[:, :], ACT.Ln).then_inc(rsq, 1)
                act.wait_ge(rsq, 2 * nb + 1)
                act.activation(y1[:, :], ln1v[:, :], ACT.Exp, scale=-0.5).then_inc(rsq, 1)

            def copy_raw(k, first):
                act.wait_ge(pv_done, NT * (k + 1))
                if not first:
                    act.wait_ge(o_scaled, k)
                act.copy(o_raw[:, :], ps_o[:, :]).then_inc(raw_copied, 1)

            def o_hi_part(part, b, g, k, gk):
                act.wait_ge(o_scaled, k + 1)
                if g == 1 and part in ("mid", "last"):
                    act.wait_ge(dense_full, number(part, b, 1, "wo3"))
                act.activation(o_hi[:, gk, :], o_sb[:, :], ACT.Identity, bias=bv[:, gk:gk + 1]).then_inc(ohi_done, 1)

            def center(pb_, st):
                act.wait_ge(ln2, 17 * pb_ + 4 * st + 3)
                act.wait_ge(xc_stored[st % 2], 16 + 16 * (NT // 2 * pb_ + st // 2))
                act.activation(xc[:, st % 2, :], h1[:, st % 2, :], ACT.Identity, bias=negm[:, st:st + 1]).then_inc(xc_ready, 1)

            def exp_unit(k, i, first):
                tt, j = i // GH, i % GH
                act.wait_ge(s2_full, UNITS * k + i + 1)
                if j == 0 and tt < NT - 1 and not first:
                    act.wait_ge(added, 3 * (k - 1) + tt + 1)
                act.activation(probs[:, tt, j, :], ps_s2[:, s2_bank(i), :], ACT.Exp).then_inc(exp_done, 1)

            for g, _, name in PROLOGUE:
                dense("prologue", 0, 0, g, name)
                if name == "h0_3":
                    rsqrt(0)

            def batch(part, b, parity):
                for g in range(GROUPS):
                    k = GROUPS * b + g
                    start = part == "first" and g == 0
                    for i in range(UNITS):
                        for name in items_at(part, g, i):
                            dense(part, b, parity, g, name)
                        if i == 3 and not start:
                            copy_raw(k - 1, part == "first" and g == 1)
                        if i == DEN + 2 and not start:
                            o_hi_part(part, b, g, k - 1, g - 1 if g else GROUPS - 1)
                        if g == 2 and i == 0 and part != "last":
                            rsqrt(b + 1)
                        if part != "first":
                            for st, at in enumerate(CENTER_AT):
                                if at == (g, i):
                                    center(b - 1, st)
                        exp_unit(k, i, start)

            act.wait_ge(w_ready, 2)
            act.wait_ge(wo_ready, 2)
            for_batches(act, batch)
            copy_raw(STEPS - 1, False)
            inverse_den("epilogue", B - 1, 0)
            o_hi_part("epilogue", B - 1, 0, STEPS - 1, GROUPS - 1)
            for st in range(NT):
                center(B - 1, st)

        @block.vector
        def _(dve):
            dve.memset(ones_mean[:, :], 1.0 / S).then_inc(consts, 1)
            dve.memset(ones_den[:, :], 1.0).then_inc(consts, 1)
            for g in range(GROUPS):
                last = dve.memset(k_stack[g][QK_ROWS:QKM_ROWS, :, :].bitcast(F32), 1.0)
            last.then_inc(consts, 1)

            dve.wait_ge(loaded, 16 * LOADS)
            two_pi = 6.283185307179586
            c1 = 6.28125
            c2 = 507.0 / 2 ** 18
            c3 = two_pi - c1 - c2
            chain = [0]

            def link(ins):
                chain[0] += 1
                ins.then_inc(trig_dve, 1)
                dve.wait_ge(trig_dve, chain[0])

            for out, phase, shift in ((cosr, 0.25, two_pi / 4), (sinr, 0.0, 0.0)):
                link(dve.tensor_scalar(turn, rot, 1.0 / two_pi, phase, ALU.mult, ALU.add))
                link(dve.tensor_scalar(red, turn, MAGIC, None, ALU.add))
                link(dve.tensor_scalar(turn, red, MAGIC, None, ALU.subtract))
                link(dve.scalar_tensor_tensor(red, turn, -c1, rot, ALU.mult, ALU.add))
                link(dve.scalar_tensor_tensor(out, turn, -c2, red, ALU.mult, ALU.add))
                link(dve.scalar_tensor_tensor(red, turn, -c3, out, ALU.mult, ALU.add))
                link(dve.tensor_scalar(turn, red, shift, 3.1415925, ALU.add, ALU.min))
                dve.tensor_scalar(out, turn, -3.1415925, None, ALU.max).then_inc(trig, 1)
                dve.wait_ge(trig, 1 if out is cosr else 2)
            dve.wait_ge(trig_act, 1)
            link(dve.scalar_tensor_tensor(red, cosr, float(DH) ** -0.5, spiral, ALU.mult, ALU.mult))
            dve.wait_ge(trig_act, 2)
            for n, scale, bias, at in (("q", red, bq, 0), ("k", sinr, bk, GROUPS)):
                dve.tensor_tensor(bias[:, :], bias_in[:, at:at + GROUPS], scale[:, S:L], ALU.mult)
                dve.tensor_tensor(w_in[n][:, :, :], w_in[n][:, :, :],
                                  scale[:, 0:S].unsqueeze(1).to_broadcast([P, NT, S]), ALU.mult).then_inc(w_ready, 1)

            def lo(part, b, g, name, out, hi_tile, bias=None, rows=slice(0, P)):
                dve.wait_ge(hi_ready, hi_number(part, b, g, name))
                bank = bank_of(part, g, name)
                src = ps_dense[bank][rows, :]
                if bias is None:
                    dve.tensor_tensor(out, src, hi_tile.bitcast(F32), ALU.subtract).then_inc(dense_done[bank], 1)
                else:
                    dve.scalar_tensor_tensor(out, src, bias, hi_tile.bitcast(F32), ALU.add, ALU.subtract).then_inc(dense_done[bank], 1)

            def dense(part, b, parity, g, name):
                nb, npar = (0, 0) if part == "prologue" else (b + 1, 1 - parity)
                bank = bank_of(part, g, name)
                ps_d = ps_dense[bank]
                if name in ("pq", "pk"):
                    gg = g if part == "prologue" else (g + 2) % GROUPS
                    hi_t, lo_t, bias = (q_hi, q_lo, bq) if name == "pq" else (k_hi, k_lo, bk)
                    lo(part, b, g, name, lo_t[:, :], hi_t[:, :], bias[:, gg:gg + 1])
                elif name == "tu":
                    lo(part, b, g, name, e_lo[npar][:, :], e_hi[npar][:, :])
                elif name == "tr":
                    lo(part, b, g, name, x_stk[E_DIM:P, :], x_hi[E_DIM:P, :], rows=slice(E_DIM, P))
                elif name in ("aq", "ak", "av"):
                    lo(part, b, g, name, a_lo[name[1]][:, :], a_hi[name[1]][:, :])
                elif name == "mt":
                    lo(part, b, g, name, m_parts[DH:DH + GH, :], m_parts[0:GH, :], rows=slice(0, GH))
                elif name == "mean":
                    dve.wait_ge(dense_full, number(part, b, g, name))
                    dve.tensor_tensor(cent2[:, :, :, :], emb[:, :, :].unsqueeze(2).to_broadcast([P, NT, 2, E_DIM]),
                                      ps_d[:, 0:E_DIM].unsqueeze(1).unsqueeze(1).to_broadcast([P, NT, 2, E_DIM]),
                                      ALU.subtract).then_inc(dense_done[bank], 1)
                elif name.startswith("h0_"):
                    st = int(name[3])
                    dve.wait_ge(dense_full, number(part, b, g, name))
                    dve.bn_stats(bn1[:, st, :], ps_d[:, :]).then_inc(dense_done[bank], 1)
                    if st == NT - 1:
                        variance(part, b, g, nb)
                elif name in WO:
                    h1_rows(ps_d, bank, part, b, g, int(name[2]))

            def variance(part, b, g, nb):
                wait_done(dve, part, b, g, "h0_3")
                stand_alone(dve, dve_waited)
                for st in range(NT):
                    dve.bn_aggr(mv1[:, st, :], bn1[:, st, :]).then_inc(ln1, 1)
                dve.wait_ge(ln1, 10 * nb + 4)
                dve.tensor_scalar(ve1[:, :], mv1[:, :, 1], EPS, None, ALU.add).then_inc(ln1, 1)

            def newton(nb):
                dve.wait_ge(rsq, 2 * (nb + 1))
                dve.tensor_tensor(t1[:, :], y1[:, :], y1[:, :], ALU.mult).then_inc(ln1, 1)
                dve.wait_ge(ln1, 10 * nb + 6)
                dve.tensor_tensor(ln1v[:, :], t1[:, :], ve1[:, :], ALU.mult).then_inc(ln1, 1)
                dve.wait_ge(ln1, 10 * nb + 7)
                dve.tensor_scalar(t1[:, :], ln1v[:, :], -0.5, 1.5, ALU.mult, ALU.add).then_inc(ln1, 1)
                dve.wait_ge(ln1, 10 * nb + 8)
                dve.scalar_tensor_tensor(r8[:, :], y1[:, :], 0.125, t1[:, :], ALU.mult, ALU.mult).then_inc(ln1, 1)
                dve.wait_ge(ln1, 10 * nb + 9)
                dve.tensor_tensor(emb2[:, :, :, :], emb[:, :, :].unsqueeze(2).to_broadcast([P, NT, 2, E_DIM]),
                                  r8[:, :].unsqueeze(2).unsqueeze(2).to_broadcast([P, NT, 2, E_DIM]),
                                  ALU.mult).then_inc(ln1, 1)

            def row_max(k, g, u):
                dve.wait_ge(s1_full, UNITS * k + u + 1)
                j, st = u // NT, u % NT
                dve.tensor_reduce(negmax[:, g % 2, st, j:j + 1], ps_s1[:, u % 2, :], AX_X, ALU.max, negate=True).then_inc(max_done, 1)

            def scale_o(k):
                dve.wait_ge(rden, k + 1)
                dve.wait_ge(raw_copied, k + 1)
                dve.tensor_tensor(o_sb[:, :], o_raw[:, :], o_sb[:, :], ALU.mult).then_inc(o_scaled, 1)

            def o_lo_part(k, gk):
                dve.wait_ge(ohi_done, k + 1)
                dve.scalar_tensor_tensor(o_lo[:, gk, :], o_sb[:, :], bv[:, gk:gk + 1], o_hi[:, gk, :].bitcast(F32),
                                         ALU.add, ALU.subtract).then_inc(olo_done, 1)

            def h1_rows(ps_d, bank, part, b, g, st):
                pb_ = B - 1 if part == "epilogue" else b - 1
                if st:
                    centered_max(pb_, st - 1)
                dve.wait_ge(dense_full, number(part, b, g, f"wo{st}"))
                dve.tensor_tensor(h1[:, st % 2, :], ps_d[:, :], bo[:, :], ALU.add).then_inc(dense_done[bank], 1)
                wait_done(dve, part, b, g, f"wo{st}")
                dve.bn_stats(bn2[:, :], h1[:, st % 2, :]).then_inc(ln2, 1)
                dve.wait_ge(ln2, 17 * pb_ + 4 * st + 1)
                stand_alone(dve, dve_waited)
                dve.bn_aggr(mv2[:, st, 0:2], bn2[:, :]).then_inc(ln2, 1)
                dve.wait_ge(ln2, 17 * pb_ + 4 * st + 2)
                dve.tensor_scalar(negm[:, st:st + 1], mv2[:, st, 0:1], -1.0, None, ALU.mult).then_inc(ln2, 1)

            def centered_max(pb_, st):
                dve.wait_ge(xc_ready, NT * pb_ + st + 1)
                dve.tensor_reduce(mv2[:, st, 2:3], xc[:, st % 2, :], AX_X, ALU.max, apply_absolute_value=True).then_inc(ln2, 1)

            def keep_stats(pb_):
                dve.wait_ge(ln2, 17 * pb_ + 16)
                dve.tensor_copy(stats[:, bass.ds(12 * pb_, 12)], mv2[:, :, :].rearrange("p t c -> p (t c)")).then_inc(ln2, 1)

            for g, _, name in PROLOGUE:
                if name == "aq":
                    dve.wait_ge(wo_loaded, 16)
                    dve.wait_ge(wo_ready, 1)
                    dve.tensor_tensor(wo_lo[:, :, :], wo_stage, wo_hi[:, :, :].bitcast(F32), ALU.subtract).then_inc(wo_ready, 1)
                if name == "tr":
                    newton(0)
                if name == "av":
                    for u in range(UNITS):
                        row_max(0, 0, u)
                dense("prologue", 0, 0, g, name)
            for u in range(AHEAD):
                row_max(1, 1, u)

            def batch(part, b, parity):
                for g in range(GROUPS):
                    k = GROUPS * b + g
                    start = part == "first" and g == 0
                    for i in range(UNITS):
                        u = i + AHEAD
                        if u < UNITS and not (part == "last" and g + 1 >= GROUPS):
                            row_max(k + 1, (g + 1) % GROUPS, u)
                        if u >= UNITS and not (part == "last" and g + 2 >= GROUPS):
                            row_max(k + 2, (g + 2) % GROUPS, u - UNITS)
                        for name in items_at(part, g, i):
                            dense(part, b, parity, g, name)
                        if i == DEN + 1 and not start:
                            scale_o(k - 1)
                        if i == DEN + 3 and not start:
                            o_lo_part(k - 1, g - 1 if g else GROUPS - 1)
                        if g == 2 and i == 1 and part != "last":
                            newton(b + 1)
                        if g == 1 and i == 8 and part != "first":
                            centered_max(b - 1, NT - 1)
                            keep_stats(b - 1)

            for_batches(dve, batch)
            scale_o(STEPS - 1)
            o_lo_part(STEPS - 1, GROUPS - 1)
            for st in range(NT):
                dense("epilogue", B - 1, 1, 0, f"wo{st}")
            centered_max(B - 1, NT - 1)
            keep_stats(B - 1)

        @block.gpsimd
        def _(pool):
            pool.memset(ident[:, :], 0.0).then_inc(pool_const, 1)
            pool.wait_ge(pool_const, 1)
            pool.affine_select(out=ident[:, :], in_=ident[:, :], compare_op=ALU.not_equal, fill=1.0, base=0,
                               pattern=[[-1, P]], channel_multiplier=1).then_inc(pool_const, 1)

            def gather(nb, first):
                pool.wait_ge(ids_loaded, 16 * (nb + 1))
                if not first:
                    pool.wait_ge(ln1, 10 * nb)
                    pool.wait_ge(emb2_ready, nb)
                    stand_alone(pool, pool_waited)
                for tt in range(NT):
                    pool.indirect_dma_start(emb[:, tt, :], None, d["table"],
                                            bass.IndirectOffsetOnAxis(ap=ids[:, tt:tt + 1].bitcast(U32), axis=0)).then_inc(gathered, 16)

            def double(part, b, nb, first):
                pool.wait_ge(gathered, 16 * NT * (nb + 1))
                if not first:
                    if part == "first":
                        pool.wait_ge(dense_full, number("prologue", 0, 0, "tr"))
                    else:
                        pool.wait_ge(dense_full, number("mid", b - 1, 2, "tr"))
                stand_alone(pool, pool_waited)
                pool.tensor_scalar(emb2[:, :, :, :], emb[:, :, :].unsqueeze(2).to_broadcast([P, NT, 2, E_DIM]),
                                   1.0, 0.0, ALU.mult, ALU.add).then_inc(emb2_ready, 1)

            def stack_e(part, b, g, nb, par):
                pool.wait_ge(hi_ready, hi_number(part, b, g, "tu"))
                stand_alone(pool, pool_waited)
                pool.tensor_scalar(e_stk8[par][0:E_DIM, :], e_hi[par][0:E_DIM, :].bitcast(F32), 0.125, 0.0,
                                   ALU.mult, ALU.add).then_inc(stk8_ready, 1)
                wait_done(pool, part, b, g, "tu")
                pool.wait_ge(stk8_ready, 2 * nb + 1)
                if part != "prologue":
                    pool.wait_ge(added, 3 * (GROUPS * b + 1))
                stand_alone(pool, pool_waited)
                pool.tensor_scalar(e_stk8[par][E_DIM:P, :], e_lo[par][E_DIM:P, :].bitcast(F32), 0.125, 0.0,
                                   ALU.mult, ALU.add).then_inc(stk8_ready, 1)
                pool.wait_ge(stk8_ready, 2 * (nb + 1))

            def stack_x(part, b, g, nb):
                pool.wait_ge(hi_ready, hi_number(part, b, g, "tr"))
                stand_alone(pool, pool_waited)
                pool.tensor_scalar(x_stk[0:E_DIM, :], x_hi[0:E_DIM, :].bitcast(F32), 1.0, 0.0,
                                   ALU.mult, ALU.add).then_inc(xtop_ready, 1)

            def add(k, a):
                pool.wait_ge(pv_done, NT * k + a + 2)
                if a:
                    pool.wait_ge(added, 3 * k + a)
                pool.tensor_tensor(probs[:, a + 1, :, :], probs[:, a, :, :], probs[:, a + 1, :, :], ALU.add).then_inc(added, 1)

            gather(0, True)
            double("prologue", 0, 0, True)
            stack_e("prologue", 0, 0, 0, 0)
            stack_x("prologue", 0, 0, 0)

            def batch(part, b, parity):
                for g in range(GROUPS):
                    k = GROUPS * b + g
                    if not (part == "first" and g == 0):
                        add(k - 1, 2)
                    if g == 1 and part != "last":
                        double(part, b, b + 1, False)
                    if g == 1 and part != "last":
                        stack_e(part, b, g, b + 1, 1 - parity)
                    if g == 2 and part != "last":
                        stack_x(part, b, g, b + 1)
                    add(k, 0)
                    add(k, 1)
                    if g == 0 and part != "last":
                        gather(b + 1, False)

            for_batches(pool, batch)
            add(STEPS - 1, 2)


def linear_block(nc, d, xc_dram, stats, out):
    with ExitStack() as ctx:
        def sb(name, shape, dt=F32):
            return ctx.enter_context(nc.sbuf_tensor("lin_" + name, shape, dt))

        def pb(name, shape, dt=F32):
            return ctx.enter_context(nc.psum_tensor("lin_" + name, shape, dt))

        def sem(name):
            return ctx.enter_context(nc.semaphore("lin_" + name))

        TILES = B * NT
        BUFS = 4
        wf = sb("wf", [P, NT, S])
        wf_y, wf_c = sb("wf_y", [P, NT, S]), sb("wf_c", [P, NT, S])
        wf_q = sb("wf_q", [P, NT, S], BF16)
        fb = sb("fb", [P, S])
        fb_r = sb("fb_r", [P, S])
        fb_h = sb("fb_h", [P, S], BF16)
        fb3 = sb("fb3", [3 * DH, S], BF16)
        sel3 = sb("sel3", [3 * DH, P], BF16)
        identb = sb("identb", [P, P], BF16)
        row = {n: sb(n, [P, TILES]) for n in ("f_ve", "f_ln", "f_y", "f_t", "f_t2", "f_r")}
        a_mean = sb("a_mean", [P, B, 2, NT])
        cur = sb("cur", [P, BUFS, 2, NT])
        am, amr = sb("am", [P, 2]), sb("amr", [P, 2])
        sc = sb("sc", [P, 8])
        x = [sb(f"x{i}", [P, NT, S]) for i in range(BUFS)]
        y = [sb(f"y{i}", [P, NT, S]) for i in range(2)]
        c = [sb(f"c{i}", [P, NT, S]) for i in range(2)]
        q = [sb(f"q{i}", [P, NT, S], BF16) for i in range(2)]
        qt = [sb(f"qt{i}", [P, NT, S], BF16) for i in range(2)]
        o = [sb(f"o{i}", [P, NT, S]) for i in range(2)]
        ps_t = pb("ps_t", [P, NT, 2 * S], BF16)
        ps_f = pb("ps_f", [P, NT, S])

        w_loaded, fb_loaded = sem("w_loaded"), sem("fb_loaded")
        x_loaded = [sem(f"x_loaded{i}") for i in range(BUFS)]
        f_const = sem("f_const")
        f_dve, f_act, f_pool = sem("f_dve"), sem("f_act"), sem("f_pool")
        wq_done = sem("wq_done")
        set_up = sem("set_up")
        cur_ready = sem("cur_ready")
        y_ready = sem("y_ready")
        r_ready = sem("r_ready")
        masked = sem("masked")
        c_ready = sem("c_ready")
        rounded = sem("rounded")
        q_ready = sem("q_ready")
        turned = sem("turned")
        qt_ready = sem("qt_ready")
        f_full = sem("f_full")
        o_ready = sem("o_ready")
        stored = [sem(f"stored{i}") for i in range(2)]

        def iterations(eng, body):
            for it in range(4):
                body(it, it)
            with eng.Fori(1, B // 4 - 1) as four:
                i = eng.snap(four * 4)
                for m in range(4):
                    body(i + m, 4 + m, True)
            for it in range(B - 4, B + 2):
                body(it, it)

        def stages(it, m, mid):
            return [(it - n if mid or 0 <= it - n < B else None) for n in range(3)]

        block = ctx.enter_context(nc.Block())

        @block.sync
        def _(sp):
            sp.dma_start(wf[:, :, :], d["wf"].rearrange("(t p) n -> p t n", p=P)).then_inc(w_loaded, 16)
            sp.dma_start(fb[:, :], d["fb_row"].partition_broadcast(P).rearrange("p a n -> p (a n)")).then_inc(fb_loaded, 16)

            def load(b, i, n):
                sp.dma_start(x[i][:, :, :], xc_dram[b].rearrange("t p n -> p t n")).then_inc(x_loaded[i], 16)

            load(0, 0, 0)
            load(1, 1, 0)

            def body(it, m, mid=False):
                a, _, cc = stages(it, m, mid)
                if mid or it + 2 < B:
                    if mid or it + 2 >= BUFS:
                        sp.wait_ge(o_ready, NT * (it - 1))
                    load(it + 2, (m + 2) % BUFS, 0)
                if cc is not None:
                    sp.wait_ge(o_ready, NT * (cc + 1))
                    sp.dma_start(out[cc].rearrange("(t p) n -> p t n", p=P), o[m % 2][:, :, :]).then_inc(stored[m % 2], 16)

            iterations(sp, body)
            for i in range(2):
                sp.wait_ge(stored[i], 16 * B // 2)

        @block.scalar
        def _(act):
            act.wait_ge(f_dve, 1)
            act.activation(row["f_ln"][:, :], row["f_ve"][:, :], ACT.Ln).then_inc(f_act, 1)
            act.wait_ge(f_act, 1)
            act.activation(row["f_y"][:, :], row["f_ln"][:, :], ACT.Exp, scale=-0.5).then_inc(f_act, 1)

            def body(it, m, mid=False):
                a, bb, _ = stages(it, m, mid)
                if a is not None:
                    act.wait_ge(x_loaded[m % BUFS], 16 * ((it - m % BUFS) // BUFS + 1) if not mid else x_count(it, m))
                    act.wait_ge(cur_ready, it + 1)
                    if mid or it >= 2:
                        act.wait_ge(q_ready, it - 1)
                    for st in range(NT):
                        act.activation(y[m % 2][:, st, :], x[m % BUFS][:, st, :], ACT.Identity,
                                       scale=cur[:, m % BUFS, 0, st:st + 1]).then_inc(y_ready, 1)
                if bb is not None:
                    for st in range(NT):
                        act.wait_ge(turned, NT * bb + st + 1)
                        if st == 0 and (mid or bb >= 2):
                            act.wait_ge(f_full, NT * (bb - 1))
                        act.copy(qt[(m + 1) % 2][:, st, :], ps_t[:, st, 0:S]).then_inc(qt_ready, 1)
                if a is not None:
                    act.wait_ge(y_ready, NT * (it + 1))
                    for st in range(NT):
                        act.activation(x[m % BUFS][:, st, :], x[m % BUFS][:, st, :], ACT.Identity,
                                       bias=cur[:, m % BUFS, 1, st:st + 1]).then_inc(r_ready, 1)

            def x_count(it, m):
                return (it - m % BUFS) * (16 // BUFS) + 16

            iterations(act, body)

        @block.vector
        def _(dve):
            steps = [0]

            def link(ins):
                steps[0] += 1
                ins.then_inc(f_dve, 1)
                dve.wait_ge(f_dve, steps[0])

            st3 = stats[:, :].rearrange("p (t c) -> p t c", c=3)
            link(dve.tensor_scalar(row["f_ve"][:, :], st3[:, :, 1], EPS, None, ALU.add))
            dve.memset(identb[:, :], 0.0).then_inc(f_const, 1)
            link(dve.memset(sel3[:, :], 0.0))
            for i in range(3):
                link(dve.memset(sel3[i * DH:i * DH + 1, :], 1.0))
            dve.wait_ge(f_act, 2)
            link(dve.tensor_tensor(row["f_t"][:, :], row["f_y"][:, :], row["f_y"][:, :], ALU.mult))
            link(dve.tensor_tensor(row["f_t2"][:, :], row["f_t"][:, :], row["f_ve"][:, :], ALU.mult))
            link(dve.tensor_scalar(row["f_t"][:, :], row["f_t2"][:, :], -0.5, 1.5, ALU.mult, ALU.add))
            link(dve.tensor_tensor(row["f_r"][:, :], row["f_y"][:, :], row["f_t"][:, :], ALU.mult))
            link(dve.tensor_tensor(row["f_t"][:, :], row["f_r"][:, :], st3[:, :, 2], ALU.mult))
            link(dve.tensor_reduce(am[:, 0:1], row["f_t"][:, :], AX_X, ALU.max))
            dve.wait_ge(w_loaded, 16)
            link(dve.tensor_reduce(am[:, 1:2], wf[:, :, :].rearrange("p t n -> p (t n)"), AX_X, ALU.max, apply_absolute_value=True))
            dve.tensor_copy(amr[:, :], am[:, :]).then_inc(set_up, 1)
            dve.wait_ge(f_pool, 3)
            link(dve.tensor_scalar(sc[:, 0:1], amr[:, 0:1], 1.0 / FP8_RANGE, None, ALU.mult))
            link(dve.tensor_tensor(sc[:, 6:7], amr[:, 0:1], amr[:, 1:2], ALU.max))
            link(dve.tensor_scalar(sc[:, 1:2], sc[:, 6:7], 1.0 / FP8_RANGE, None, ALU.mult))
            link(dve.reciprocal(sc[:, 2:4], sc[:, 0:2]))
            link(dve.tensor_tensor(sc[:, 4:5], sc[:, 0:1], sc[:, 1:2], ALU.mult))
            link(dve.reciprocal(sc[:, 5:6], sc[:, 4:5]))
            link(dve.tensor_scalar(a_mean[:, :, 0, :], row["f_r"][:, :].rearrange("p (b t) -> p b t", t=NT), sc[:, 2:3], None, ALU.mult))
            link(dve.tensor_copy(a_mean[:, :, 1, :], st3[:, :, 0].rearrange("p (b t) -> p b t", t=NT)))

            def mask(out, src):
                return dve.tensor_scalar(out.bitcast(U32), src.bitcast(U32), 0x7F800000, None, ALU.bitwise_and)

            def shifter(out, src):
                return dve.tensor_scalar(out, src, 2.0 ** -6, 1.5 * 2.0 ** 20, ALU.max, ALU.mult)

            link(dve.tensor_scalar(wf_y[:, :, :], wf[:, :, :], sc[:, 3:4], None, ALU.mult))
            link(mask(wf_c[:, :, :], wf_y[:, :, :]))
            link(shifter(wf_c[:, :, :], wf_c[:, :, :]))
            link(dve.tensor_tensor(wf_y[:, :, :], wf_y[:, :, :], wf_c[:, :, :], ALU.add))
            link(dve.tensor_tensor(wf_q[:, :, :], wf_y[:, :, :], wf_c[:, :, :], ALU.subtract))
            dve.wait_ge(fb_loaded, 16)
            link(dve.tensor_scalar(fb_r[:, :], fb[:, :], sc[:, 5:6], None, ALU.mult))
            link(dve.tensor_copy(fb_h[:, :], fb_r[:, :]))
            link(dve.tensor_copy(fb3[0:DH, :], fb_r[0:DH, :]))
            link(dve.tensor_tensor(fb[:, :], fb_r[:, :], fb_h[:, :], ALU.subtract))
            link(dve.tensor_copy(fb3[DH:2 * DH, :], fb[DH:2 * DH, :]))
            link(dve.tensor_copy(fb_h[:, :], fb[:, :]))
            link(dve.tensor_tensor(fb_r[:, :], fb[:, :], fb_h[:, :], ALU.subtract))
            dve.tensor_copy(fb3[2 * DH:3 * DH, :], fb_r[2 * DH:3 * DH, :]).then_inc(wq_done, 1)

            def body(it, m, mid=False):
                a, bb, cc = stages(it, m, mid)
                if a is not None:
                    dve.tensor_copy(cur[:, m % BUFS, :, :].rearrange("p c t -> p (c t)"),
                                    a_mean[:, :, :, :].rearrange("p b c t -> p (b c t)")[:, bass.ds(2 * NT * it, 2 * NT)]).then_inc(cur_ready, 1)
                if cc is not None:
                    for st in range(NT):
                        dve.wait_ge(f_full, NT * cc + st + 1)
                        if st == 0:
                            dve.wait_ge(r_ready, NT * (cc + 1))
                            if mid or cc >= 2:
                                dve.wait_ge(stored[m % 2], 8 * (cc - m % 2))
                        dve.scalar_tensor_tensor(o[m % 2][:, st, :], ps_f[:, st, :], sc[:, 4:5], x[(m - 2) % BUFS][:, st, :],
                                                 ALU.mult, ALU.add).then_inc(o_ready, 1)
                if bb is not None:
                    dve.wait_ge(rounded, bb + 1)
                    if mid or bb >= 2:
                        dve.wait_ge(turned, NT * (bb - 1))
                    dve.tensor_tensor(q[(m + 1) % 2][:, :, :], y[(m + 1) % 2][:, :, :], c[(m + 1) % 2][:, :, :],
                                      ALU.subtract).then_inc(q_ready, 1)
                if a is not None:
                    dve.wait_ge(y_ready, NT * (it + 1))
                    if mid or it >= 2:
                        dve.wait_ge(q_ready, it - 1)
                    mask(c[m % 2][:, :, :], y[m % 2][:, :, :]).then_inc(masked, 1)
                    dve.wait_ge(masked, it + 1)
                    shifter(c[m % 2][:, :, :], c[m % 2][:, :, :]).then_inc(c_ready, 1)

            iterations(dve, body)

        @block.gpsimd
        def _(pool):
            pool.wait_ge(f_const, 1)
            pool.affine_select(out=identb[:, :], in_=identb[:, :], compare_op=ALU.not_equal, fill=1.0, base=0,
                               pattern=[[-1, P]], channel_multiplier=1).then_inc(f_pool, 1)
            pool.wait_ge(set_up, 1)
            pool.partition_all_reduce(amr[:, 0:1], am[:, 0:1], P, bass.bass_isa.ReduceOp.max).then_inc(f_pool, 1)
            pool.partition_all_reduce(amr[:, 1:2], am[:, 1:2], P, bass.bass_isa.ReduceOp.max).then_inc(f_pool, 1)

            def body(it, m, mid=False):
                a, _, _ = stages(it, m, mid)
                if a is not None:
                    pool.wait_ge(c_ready, it + 1)
                    pool.tensor_tensor(y[m % 2][:, :, :], y[m % 2][:, :, :], c[m % 2][:, :, :], ALU.add).then_inc(rounded, 1)

            iterations(pool, body)

        @block.tensor
        def _(pe):
            pe.wait_ge(f_pool, 1)
            pe.wait_ge(wq_done, 1)

            def body(it, m, mid=False):
                _, bb, _ = stages(it, m, mid)
                if bb is None:
                    return
                pe.wait_ge(q_ready, bb + 1)
                for st in range(NT):
                    if mid or bb >= 1:
                        pe.wait_ge(qt_ready, NT * (bb - 1) + st + 1)
                    for ib in range(NT):
                        last = pe.transpose(ps_t[:, st, ib * P:(ib + 1) * P], q[(m + 1) % 2][:, st, ib * P:(ib + 1) * P], identb[:, :])
                    last.then_inc(turned, 1)
                for st in range(NT):
                    pe.wait_ge(qt_ready, NT * bb + st + 1)
                    if mid or bb >= 1:
                        pe.wait_ge(o_ready, NT * (bb - 1) + st + 1)
                    pe.matmul(ps_f[:, st, :], sel3[:, :], fb3[:, :], start=True, stop=False)
                    for ib in range(NT):
                        last = pe.matmul(ps_f[:, st, :], qt[(m + 1) % 2][:, st, ib * P:(ib + 1) * P], wf_q[:, ib, :],
                                         start=False, stop=(ib == NT - 1))
                    last.then_inc(f_full, 1)

            iterations(pe, body)


def tower(nc, d, out):
    with ExitStack() as ctx:
        stats = ctx.enter_context(nc.sbuf_tensor("stats", [P, B * NT * 3], F32))
        xc_dram = nc.dram_tensor("xc_dram", (B, NT, P, S), F32, kind="Internal").ap()
        attention_block(nc, d, xc_dram, stats)
        linear_block(nc, d, xc_dram, stats, out)


def kernel(**inputs):
    import numpy as np
    from concourse import bacc
    from concourse.bass_utils import run_bass_kernel_spmd

    nc = bacc.Bacc("TRN2", target_bir_lowering=False, num_devices=1, dynamic_dma_scratch_size=4096)
    a = {n: np.asarray(v) for n, v in inputs.items()}

    def by_dim(v):
        return v.reshape((GROUPS, GH, DH) + v.shape[1:]).swapaxes(1, 2).reshape(v.shape)

    def cols(v):
        return v.reshape(GROUPS, P).T

    rot = by_dim(a["L0_attn_helix_rotation"])
    spiral = by_dim(np.repeat(a["L0_attn_spiral_weight"], DH))
    arrays = {
        "ids": a["x"].reshape(B, NT, P).swapaxes(1, 2),
        "table": a["L0_tok_weight"],
        "wq": by_dim(a["L0_attn_Wq"]).T, "wk": by_dim(a["L0_attn_Wk"]).T, "wv": a["L0_attn_Wv"].T,
        "wo": a["L0_attn_Wo"].T, "wf": a["L0_ffn_weight"].T,
        "bq_col": cols(by_dim(a["L0_attn_bq"])), "bk_col": cols(by_dim(a["L0_attn_bk"])), "bv_col": cols(a["L0_attn_bv"]),
        "bo_row": a["L0_attn_bo"][None], "fb_row": a["L0_ffn_bias"][None],
        "rot_row": rot[None], "rot_col": cols(rot), "spiral_row": spiral[None], "spiral_col": cols(spiral),
    }
    arrays = {f"in_{n}": np.ascontiguousarray(v) for n, v in arrays.items()}
    d = {n[3:]: nc.dram_tensor(n, v.shape, mybir.dt.from_np(v.dtype), kind="ExternalInput").ap() for n, v in arrays.items()}
    out = nc.dram_tensor("out", (B, S, S), F32, kind="ExternalOutput").ap()
    tower(nc, d, out)
    r = run_bass_kernel_spmd(nc, [arrays], core_ids=[0])
    return r.results[0]["out"]
```

```python
from contextlib import ExitStack

import concourse.bass as bass
from concourse import mybir

ALU = mybir.AluOpType
ACT = mybir.ActivationFunctionType
AX_X = mybir.AxisListType.X
F32 = mybir.dt.float32
F32R = mybir.dt.float32r
BF16 = mybir.dt.bfloat16
I32 = mybir.dt.int32
U32 = mybir.dt.uint32

P = 128
B = 16
S = 512
E_DIM = 64
HEADS = 16
DH = S // HEADS
GH = 4
GROUPS = HEADS // GH
NT = S // P
STEPS = B * GROUPS
UNITS = GH * NT
DENSE_BANKS = 3
S2_BANKS = 2
AHEAD = 5
QK_ROWS = 3 * DH
QKM_ROWS = QK_ROWS + 2
EPS = 1e-5
FP8_RANGE = 448.0 * 0.8
MAGIC = 1.5 * 2.0 ** 23

DEN = 8
MID = [(0, 0, "v0"), (0, 1, "pq"), (0, 4, "v1"), (0, 5, "pk"), (0, 7, "v2"), (0, DEN, "den"), (0, 12, "v3"),
       (0, 13, "wo0"), (0, 13, "mt"), (0, 15, "wo1"),
       (1, 1, "pq"), (1, 2, "wo2"), (1, 3, "pk"), (1, 5, "wo3"), (1, 7, "mean"), (1, 7, "tu"),
       (1, DEN, "den"), (1, 10, "h0_0"), (1, 11, "aq"), (1, 11, "h0_1"), (1, 12, "mt"), (1, 12, "h0_2"),
       (1, 13, "h0_3"), (1, 15, "ak"),
       (2, 0, "tr"), (2, 3, "pq"), (2, 5, "pk"), (2, DEN, "den"), (2, 12, "mt"),
       (3, 0, "pq"), (3, 3, "pk"), (3, 5, "av"), (3, DEN, "den"), (3, 13, "mt")]
CENTER_AT = ((0, 13), (1, 0), (1, 3), (1, 6))
PREPARE = ("mean", "tu", "h0_0", "h0_1", "h0_2", "h0_3", "aq", "tr", "ak", "av")
WO = ("wo0", "wo1", "wo2", "wo3")
FIRST = [x for x in MID if x[2] not in WO and x[::2] != (0, "den")]
LAST = [x for x in MID if x[2] not in PREPARE and not (x[0] >= 2 and x[2] in ("pq", "pk")) and x[::2] != (3, "mt")]
PROLOGUE = [(0, 0, n) for n in ("mean", "tu", "h0_0", "h0_1", "h0_2", "h0_3", "tr", "aq", "ak")] + [
    (0, 0, "pq"), (0, 0, "pk"), (1, 0, "pq"), (1, 0, "pk"), (0, 0, "av"), (0, 0, "mt")]
EPILOGUE = [(0, 0, "den")] + [(0, 0, n) for n in WO]
ITEMS = {"prologue": PROLOGUE, "first": FIRST, "mid": MID, "last": LAST, "epilogue": EPILOGUE}
HI = ("pq", "pk", "mt", "tu", "tr", "aq", "ak", "av")


def bank_of(part, g, name):
    return [x[::2] for x in ITEMS[part]].index((g, name)) % DENSE_BANKS


def count(part, b, g, name, counts):
    def size(p, upto=None):
        return sum(1 for gg, _, n in ITEMS[p][:upto] if counts(p, gg, n))

    here = size(part, [x[::2] for x in ITEMS[part]].index((g, name)) + 1)
    if part == "prologue":
        return here
    if part == "first":
        return size("prologue") + here
    base = size("prologue") + size("first")
    if part == "mid":
        return base + (b - 1) * size("mid") + here
    base += (B - 2) * size("mid")
    return base + here if part == "last" else base + size("last") + here


def number(part, b, g, name):
    return count(part, b, g, name, lambda *x: True)


def hi_number(part, b, g, name):
    return count(part, b, g, name, lambda p, gg, n: n in HI)


def bank_number(part, b, g, name):
    bank = bank_of(part, g, name)
    return count(part, b, g, name, lambda p, gg, n: bank_of(p, gg, n) == bank)


def s2_bank(i):
    return 1 if i == UNITS - 1 and UNITS % S2_BANKS == 1 else i % S2_BANKS


def s2_back(i):
    return next(n for n in range(1, UNITS + 1) if s2_bank((i - n) % UNITS) == s2_bank(i))


def items_at(part, g, slot):
    return [n for gg, ss, n in ITEMS[part] if gg == g and ss == slot]


def for_batches(eng, body):
    body("first", 0, 0)
    with eng.Fori(0, (B - 2) // 2) as pair:
        b = eng.snap(pair * 2 + 1)
        body("mid", b, 1)
        body("mid", b + 1, 0)
    body("last", B - 1, 1)


def stand_alone(eng, sem):
    eng.sem_inc(sem, 1)


def attention_block(nc, d, xc_dram, stats):
    with ExitStack() as ctx:
        def sb(name, shape, dt=F32):
            return ctx.enter_context(nc.sbuf_tensor(name, shape, dt))

        def pb(name, shape):
            return ctx.enter_context(nc.psum_tensor(name, shape, F32))

        def sem(name):
            return ctx.enter_context(nc.semaphore(name))

        w_in = {n: sb(f"w_{n}", [P, NT, S]) for n in "qkv"}
        wo_hi, wo_lo = sb("wo_hi", [P, NT, S], F32R), sb("wo_lo", [P, NT, S], F32R)
        bq, bk, bv = sb("bq", [P, GROUPS]), sb("bk", [P, GROUPS]), sb("bv", [P, GROUPS])
        bo_stk = sb("bo_stk", [P, S], F32R)
        mean_64 = sb("mean_64", [P, P], F32R)
        ones_mean = sb("ones_mean", [P, P])
        ones_den = sb("ones_den", [P, DH])
        ident = sb("ident", [P, P])
        q_stack = [sb(f"q_stack{g}", [P, GH, S], F32R) for g in range(GROUPS)]
        k_stack = [sb(f"k_stack{g}", [P, GH, S], F32R) for g in range(GROUPS)]
        q_hi, q_lo = sb("q_hi", [P, S], F32R), sb("q_lo", [P, S], F32R)
        k_hi, k_lo = sb("k_hi", [P, S], F32R), sb("k_lo", [P, S], F32R)
        v_sb = sb("v_sb", [P, NT, S])
        probs = sb("probs", [P, NT, GH, S])
        o_raw, o_sb = sb("o_raw", [P, S]), sb("o_sb", [P, S])
        o_hi, o_lo = sb("o_hi", [P, GROUPS, S], F32R), sb("o_lo", [P, GROUPS, S], F32R)
        xc = sb("xc", [P, 2, S])
        negmax = sb("negmax", [P, 2, NT, GH])
        m_parts = sb("m_parts", [DH + GH, S], F32R)
        ids = sb("ids", [P, NT], I32)
        emb = sb("emb", [P, NT, E_DIM])
        emb2 = sb("emb2", [P, NT, 2, E_DIM])
        cent = sb("cent", [P, NT, E_DIM])
        e_hi = [sb(f"e_hi{i}", [P, S], F32R) for i in range(2)]
        e_lo = [sb(f"e_lo{i}", [P, S], F32R) for i in range(2)]
        e_stk8 = [sb(f"e_stk8_{i}", [P, S], F32R) for i in range(2)]
        x_hi = sb("x_hi", [P, S], F32R)
        x_stk = sb("x_stk", [P, S], F32R)
        a_hi = {n: sb(f"a_hi_{n}", [P, S], F32R) for n in "qkv"}
        a_lo = {n: sb(f"a_lo_{n}", [P, S], F32R) for n in "qkv"}
        bn1, mv1 = sb("bn1", [P, NT, 6]), sb("mv1", [P, NT, 2])
        ve1, ln1v, y1, t1, r8 = (sb(n, [P, NT]) for n in ("ve1", "ln1v", "y1", "t1", "r8"))
        bn2, mv2, negm = sb("bn2", [P, 6]), sb("mv2", [P, NT, 3]), sb("negm", [P, NT])

        ps_s2 = pb("ps_s2", [P, S2_BANKS, S])
        ps_s1 = pb("ps_s1", [P, 2, S])
        ps_dense = [pb(f"ps_d{i}", [P, S]) for i in range(DENSE_BANKS)]
        ps_o = pb("ps_o", [P, S])

        loaded = sem("loaded")
        rot_loaded = sem("rot_loaded")
        wo_loaded = sem("wo_loaded")
        consts = sem("consts")
        pool_const = sem("pool_const")
        trig = sem("trig")
        trig_act = sem("trig_act")
        trig_dve = sem("trig_dve")
        w_ready = sem("w_ready")
        wo_ready = sem("wo_ready")
        bo_ready = sem("bo_ready")
        ids_loaded = sem("ids_loaded")
        gathered = sem("gathered")
        emb2_ready = sem("emb2_ready")
        stk8_ready = sem("stk8_ready")
        xtop_ready = sem("xtop_ready")
        ln1 = sem("ln1")
        rsq = sem("rsq")
        dense_full = sem("dense_full")
        dense_done = [sem(f"dense_done{i}") for i in range(DENSE_BANKS)]
        hi_ready = sem("hi_ready")
        stack_loaded = sem("stack_loaded")
        m_loaded = sem("m_loaded")
        s1_full = sem("s1_full")
        max_done = sem("max_done")
        s2_full = sem("s2_full")
        exp_done = sem("exp_done")
        pv_done = sem("pv_done")
        added = sem("added")
        raw_copied = sem("raw_copied")
        rden = sem("rden")
        o_scaled = sem("o_scaled")
        ohi_done = sem("ohi_done")
        olo_done = sem("olo_done")
        ln2 = sem("ln2")
        xc_stored = [sem(f"xc_stored{i}") for i in range(2)]

        dve_waited, pool_waited = sem("dve_waited"), sem("pool_waited")

        block = ctx.enter_context(nc.Block())

        def a_parts(dst, h):
            return slice(dst * E_DIM, (dst + 1) * E_DIM), slice(h * E_DIM, (h + 1) * E_DIM), slice(h * S // 2, (h + 1) * S // 2)

        def wo_group(part, st):
            return next(g for g, _, n in ITEMS[part] if n == f"wo{st}")

        def wait_done(eng, part, b, g, name):
            eng.wait_ge(dense_done[bank_of(part, g, name)], bank_number(part, b, g, name))

        wo_stage = probs[:, 0, :, :]
        L = S + GROUPS
        flat = probs[:, 1:4, :, :].rearrange("p a h n -> p (a h n)")

        def region(i):
            return flat[:, i * L:(i + 1) * L]

        rot, spiral, cosr, sinr, turn, red = (region(i) for i in range(6))
        bias_in = region(6)
        ROT_LOADS = 4
        LOADS = 7

        @block.sync
        def _(sp):
            for i in range(2):
                sp.sem_inc(xc_stored[i], 16)
            sp.dma_start(ids[:, :], d["ids"][0]).then_inc(ids_loaded, 16)
            sp.dma_start(rot[:, 0:S], d["rot_row"].partition_broadcast(P).rearrange("p a n -> p (a n)")).then_inc(rot_loaded, 16)
            sp.dma_start(rot[:, S:L], d["rot_col"]).then_inc(rot_loaded, 16)
            sp.dma_start(spiral[:, 0:S], d["spiral_row"].partition_broadcast(P).rearrange("p a n -> p (a n)")).then_inc(rot_loaded, 16)
            sp.dma_start(spiral[:, S:L], d["spiral_col"]).then_inc(rot_loaded, 16)
            sp.dma_start(bias_in[:, 0:GROUPS], d["bq_col"]).then_inc(loaded, 16)
            sp.dma_start(bias_in[:, GROUPS:2 * GROUPS], d["bk_col"]).then_inc(loaded, 16)
            sp.wait_ge(gathered, 16 * NT)
            for n in "qkv":
                sp.dma_start(w_in[n][:, :, :], d[f"w{n}"].rearrange("(t p) n -> p t n", p=P)).then_inc(loaded, 16)
            sp.dma_start(bv[:, :], d["bv_col"]).then_inc(loaded, 16)
            sp.dma_start(o_raw[:, :], d["bo_row"].partition_broadcast(P).rearrange("p a n -> p (a n)")).then_inc(loaded, 16)
            sp.dma_start(wo_stage, d["wo"].rearrange("(t p) n -> p t n", p=P)).then_inc(wo_loaded, 16)

            def load_ids(nb):
                sp.wait_ge(gathered, 16 * NT * nb)
                sp.dma_start(ids[:, :], d["ids"][nb]).then_inc(ids_loaded, 16)

            def stack_q(part, b, g, k, slot):
                sp.wait_ge(hi_ready, hi_number(part, b, g, "pq"))
                sp.dma_start(q_stack[slot][0:DH, :, :].bitcast(F32), q_hi[:, :].bitcast(F32)).then_inc(stack_loaded, 16)
                sp.dma_start(q_stack[slot][2 * DH:3 * DH, :, :].bitcast(F32), q_hi[:, :].bitcast(F32)).then_inc(stack_loaded, 16)
                wait_done(sp, part, b, g, "pq")
                sp.dma_start(q_stack[slot][DH:2 * DH, :, :].bitcast(F32), q_lo[:, :].bitcast(F32)).then_inc(stack_loaded, 16)

            def stack_k(part, b, g, k, slot):
                sp.wait_ge(hi_ready, hi_number(part, b, g, "pk"))
                sp.dma_start(k_stack[slot][0:DH, :, :].bitcast(F32), k_hi[:, :].bitcast(F32)).then_inc(stack_loaded, 16)
                sp.dma_start(k_stack[slot][DH:2 * DH, :, :].bitcast(F32), k_hi[:, :].bitcast(F32)).then_inc(stack_loaded, 16)
                wait_done(sp, part, b, g, "pk")
                sp.dma_start(k_stack[slot][2 * DH:3 * DH, :, :].bitcast(F32), k_lo[:, :].bitcast(F32)).then_inc(stack_loaded, 16)

            def max_rows(part, b, g, slot):
                sp.wait_ge(hi_ready, hi_number(part, b, g, "mt"))
                sp.dma_start(q_stack[slot][QK_ROWS:QK_ROWS + 1, :, :].bitcast(F32), m_parts[0:GH, :].bitcast(F32)).then_inc(m_loaded, 16)
                wait_done(sp, part, b, g, "mt")
                sp.dma_start(q_stack[slot][QK_ROWS + 1:QKM_ROWS, :, :].bitcast(F32), m_parts[DH:DH + GH, :].bitcast(F32)).then_inc(m_loaded, 16)

            def store_xc(part, b, pb_, st):
                wait_done(sp, part, b, wo_group(part, st), f"wo{st}")
                sp.dma_start(xc_dram[pb_, st], xc[:, st % 2, :]).then_inc(xc_stored[st % 2], 16)

            stack_q("prologue", 0, 0, 0, 0)
            stack_k("prologue", 0, 0, 0, 0)
            stack_q("prologue", 0, 1, 1, 1)
            stack_k("prologue", 0, 1, 1, 1)
            max_rows("prologue", 0, 0, 0)

            def batch(part, b, parity):
                for g in range(GROUPS):
                    has = [n for gg, _, n in ITEMS[part] if gg == g]
                    if g == 0 and part != "last":
                        load_ids(b + 1)
                    if g == 1 and part != "first":
                        store_xc(part, b, b - 1, 1)
                    if "pq" in has:
                        stack_q(part, b, g, 4 * b + g + 2, (g + 2) % GROUPS)
                    if "pk" in has:
                        stack_k(part, b, g, 4 * b + g + 2, (g + 2) % GROUPS)
                    if g == 1 and part != "first":
                        for st in range(2, NT):
                            store_xc(part, b, b - 1, st)
                    if "mt" in has:
                        max_rows(part, b, g, (g + 1) % GROUPS)
                    if g == 0 and part != "first":
                        store_xc(part, b, b - 1, 0)

            for_batches(sp, batch)
            for st in range(NT):
                store_xc("epilogue", B - 1, B - 1, st)
            for i in range(2):
                sp.wait_ge(xc_stored[i], 16 + 16 * B * NT // 2)

        @block.tensor
        def _(pe):
            def open_dense(part, b, g, name):
                n = bank_number(part, b, g, name)
                if not (isinstance(n, int) and n == 1):
                    pe.wait_ge(dense_done[bank_of(part, g, name)], n - 1)
                return ps_dense[bank_of(part, g, name)]

            def mean(ps_d, nb):
                pe.wait_ge(gathered, 16 * NT * (nb + 1))
                for tt in range(NT):
                    last = pe.matmul(ps_d[:, 0:E_DIM], ones_mean[:, :], emb[:, tt, :], start=(tt == 0), stop=(tt == NT - 1))
                last.then_inc(dense_full, 1)

            def turn_e(ps_d, nb, scaled):
                if not scaled:
                    pe.wait_ge(emb2_ready, nb + 1)
                else:
                    pe.wait_ge(ln1, 10 * (nb + 1))
                for tt in range(NT):
                    last = pe.transpose(ps_d[:, tt * P:(tt + 1) * P], emb2[:, tt, :, :].rearrange("p c e -> p (c e)"), ident[:, :])
                last.then_inc(dense_full, 1)

            def h0_rows(ps_d, nb, par, st):
                if st == 0:
                    pe.wait_ge(stk8_ready, 2 * (nb + 1))
                w = e_stk8[par][:, st * P:(st + 1) * P]
                pe.matmul(ps_d[:, :], w, e_hi[par][:, :], start=True, stop=False)
                pe.matmul(ps_d[:, :], w, e_lo[par][:, :], start=False, stop=True).then_inc(dense_full, 1)

            def make_a(ps_d, n):
                for jt in range(NT):
                    for h in range(2):
                        last = pe.matmul(ps_d[h * E_DIM:(h + 1) * E_DIM, 0:S // 2], cent[:, jt, :],
                                         w_in[n][:, jt, h * S // 2:(h + 1) * S // 2],
                                         start=(jt == 0), stop=(jt == NT - 1), skip_group_check=True)
                last.then_inc(dense_full, 1)

            def project(ps_d, n, nb, g):
                pe.wait_ge(xtop_ready, nb + 1)
                pe.matmul(ps_d[:, :], a_hi[n][:, g * P:(g + 1) * P], x_stk[:, :], start=True, stop=False)
                pe.matmul(ps_d[:, :], a_lo[n][:, g * P:(g + 1) * P], x_stk[:, :], start=False, stop=True).then_inc(dense_full, 1)

            def project_v(ps_d, tt):
                w = x_stk[:, tt * P:(tt + 1) * P]
                pe.matmul(ps_d[:, :], w, a_hi["v"][:, :], start=True, stop=False)
                pe.matmul(ps_d[:, :], w, a_lo["v"][:, :], start=False, stop=True).then_inc(dense_full, 1)

            def turn_max(ps_d, k, g):
                pe.wait_ge(max_done, UNITS * (k + 1))
                for st in range(NT):
                    last = pe.transpose(ps_d[0:GH, st * P:(st + 1) * P], negmax[:, g % 2, st, :], ident[:, :])
                last.then_inc(dense_full, 1)

            def denominators(ps_d, k):
                pe.wait_ge(added, 3 * (k + 1))
                for j in range(GH):
                    last = pe.matmul(ps_d[j * DH:(j + 1) * DH, :], ones_den[:, :], probs[:, NT - 1, j, :], start=True, stop=True)
                last.then_inc(dense_full, 1)

            def out_proj(ps_d, par, st, groups):
                w = e_stk8[par][:, st * P:(st + 1) * P]
                if groups[0] == 0:
                    pe.matmul(ps_d[:, :], mean_64[:, :], bo_stk[:, :], start=True, stop=False)
                    pe.matmul(ps_d[:, :], w, e_hi[par][:, :], start=False, stop=False)
                    pe.matmul(ps_d[:, :], w, e_lo[par][:, :], start=False, stop=False)
                for c in groups:
                    pe.matmul(ps_d[:, :], o_hi[:, c, st * P:(st + 1) * P], wo_hi[:, c, :], start=False, stop=False)
                    pe.matmul(ps_d[:, :], o_hi[:, c, st * P:(st + 1) * P], wo_lo[:, c, :], start=False, stop=False)
                    last = pe.matmul(ps_d[:, :], o_lo[:, c, st * P:(st + 1) * P], wo_hi[:, c, :], start=False, stop=(c == GROUPS - 1))
                if groups[-1] == GROUPS - 1:
                    last.then_inc(dense_full, 1)

            def scores_st(k, g, u, first):
                if u == 0:
                    pe.wait_ge(stack_loaded, 96 * (k + 1))
                if not (first and u < 2):
                    pe.wait_ge(max_done, UNITS * k + u - 1)
                j, st = u // NT, u % NT
                pe.matmul(ps_s1[:, u % 2, :], q_stack[g][0:QK_ROWS, j, st * P:(st + 1) * P], k_stack[g][0:QK_ROWS, j, :],
                          start=True, stop=True).then_inc(s1_full, 1)

            def scores_ts(k, g, i, first):
                if i == 0:
                    pe.wait_ge(m_loaded, 32 * (k + 1))
                back = s2_back(i)
                if not (first and i < back):
                    pe.wait_ge(exp_done, UNITS * k + i - back + 1)
                tt, j = i // GH, i % GH
                pe.matmul(ps_s2[:, s2_bank(i), :], k_stack[g][0:QKM_ROWS, j, tt * P:(tt + 1) * P], q_stack[g][0:QKM_ROWS, j, :],
                          start=True, stop=True).then_inc(s2_full, 1)

            def times_v(k, g, tt, first, part=None, b=None):
                pe.wait_ge(exp_done, UNITS * k + GH * (tt + 1))
                if g == 0:
                    wait_done(pe, part, b, 0, f"v{tt}")
                if tt == 0 and not first:
                    pe.wait_ge(raw_copied, k)
                for j in range(GH):
                    h = g * GH + j
                    last = pe.matmul(ps_o[j * DH:(j + 1) * DH, :], v_sb[:, tt, h * DH:(h + 1) * DH], probs[:, tt, j, :],
                                     start=(tt == 0), stop=(tt == NT - 1), skip_group_check=True)
                last.then_inc(pv_done, 1)

            def dense(part, b, parity, g, name):
                ps_d = open_dense(part, b, g, name)
                nb, npar = (0, 0) if part == "prologue" else (b + 1, 1 - parity)
                if name == "mean":
                    mean(ps_d, nb)
                elif name == "tu":
                    turn_e(ps_d, nb, False)
                elif name == "tr":
                    turn_e(ps_d, nb, True)
                elif name.startswith("h0_"):
                    h0_rows(ps_d, nb, npar, int(name[3]))
                elif name in ("aq", "ak", "av"):
                    if name == "aq":
                        wait_done(pe, part, b, 0 if part == "prologue" else 1, "mean")
                    make_a(ps_d, name[1])
                elif name in ("pq", "pk"):
                    if (part, g) == ("prologue", 0) or (part != "prologue" and g == 2):
                        wait_done(pe, part, b, 0 if part == "prologue" else 1, "a" + name[1])
                        wait_done(pe, part, b, 0 if part == "prologue" else 2, "tr")
                    if part == "prologue":
                        project(ps_d, name[1], 0, g)
                    else:
                        project(ps_d, name[1], b + (g + 2) // GROUPS, (g + 2) % GROUPS)
                elif name[0] == "v":
                    project_v(ps_d, int(name[1]))
                elif name == "mt":
                    if part == "prologue" or (part != "last" and g == GROUPS - 1):
                        wait_done(pe, part, b, 0 if part == "prologue" else 3, "av")
                    turn_max(ps_d, 0 if part == "prologue" else GROUPS * b + g + 1, 0 if part == "prologue" else (g + 1) % GROUPS)
                elif name == "den":
                    denominators(ps_d, STEPS - 1 if part == "epilogue" else GROUPS * b + g - 1)
                else:
                    if name == "wo0":
                        pe.wait_ge(olo_done, GROUPS * b)
                    out_proj(ps_d, 1 - parity, int(name[2]), range(GROUPS))

            pe.wait_ge(consts, 3)
            pe.wait_ge(pool_const, 2)
            for g, _, name in PROLOGUE:
                if name == "aq":
                    pe.wait_ge(w_ready, 1)
                if name == "ak":
                    pe.wait_ge(w_ready, 2)
                if name == "mt":
                    for u in range(UNITS):
                        scores_st(0, 0, u, True)
                dense("prologue", 0, 0, g, name)
            pe.wait_ge(wo_ready, 2)
            pe.wait_ge(bo_ready, 2)
            pe.wait_ge(pool_const, 2 + GROUPS)
            for u in range(AHEAD):
                scores_st(1, 1, u, False)

            def batch(part, b, parity):
                for g in range(GROUPS):
                    k = GROUPS * b + g
                    for i in range(UNITS):
                        for name in items_at(part, g, i):
                            dense(part, b, parity, g, name)
                        u = i + AHEAD
                        if u < UNITS and not (part == "last" and g + 1 >= GROUPS):
                            scores_st(k + 1, (g + 1) % GROUPS, u, False)
                        if u >= UNITS and not (part == "last" and g + 2 >= GROUPS):
                            scores_st(k + 2, (g + 2) % GROUPS, u - UNITS, False)
                        scores_ts(k, g, i, part == "first" and g == 0)
                        if i == 1 and not (part == "first" and g == 0):
                            times_v(k - 1, g - 1 if g else GROUPS - 1, NT - 1, False, part, b)
                        if i in (5, 9, 13):
                            times_v(k, g, (i - 5) // 4, part == "first" and g == 0, part, b)

            for_batches(pe, batch)
            times_v(STEPS - 1, GROUPS - 1, NT - 1, False)
            pe.wait_ge(olo_done, STEPS - 1)
            early = [open_dense("epilogue", B - 1, 0, name) for name in WO[:2]]
            for st, ps_d in enumerate(early):
                out_proj(ps_d, 1, st, range(GROUPS - 1))
            dense("epilogue", B - 1, 1, 0, "den")
            pe.wait_ge(olo_done, STEPS)
            for st, ps_d in enumerate(early):
                out_proj(ps_d, 1, st, range(GROUPS - 1, GROUPS))
            for st in range(2, NT):
                out_proj(open_dense("epilogue", B - 1, 0, f"wo{st}"), 1, st, range(GROUPS))

        @block.scalar
        def _(act):
            act.wait_ge(trig, 1)
            act.activation(cosr, cosr, ACT.Sin).then_inc(trig_act, 1)
            act.wait_ge(trig, 2)
            act.activation(sinr, sinr, ACT.Sin).then_inc(trig_act, 1)
            act.preload_act_table_set("natural_log_exp_and_others")
            def hi(part, b, g, name, out, bias=None):
                act.wait_ge(dense_full, number(part, b, g, name))
                src = ps_dense[bank_of(part, g, name)][0:out.shape[0], :]
                if bias is None:
                    act.copy(out, src).then_inc(hi_ready, 1)
                else:
                    act.activation(out, src, ACT.Identity, bias=bias).then_inc(hi_ready, 1)

            def dense(part, b, parity, g, name):
                nb, npar = (0, 0) if part == "prologue" else (b + 1, 1 - parity)
                if name in ("pq", "pk"):
                    gg = g if part == "prologue" else (g + 2) % GROUPS
                    kk = g if part == "prologue" else GROUPS * b + g + 2
                    if not (part == "prologue" and g == 0):
                        act.wait_ge(stack_loaded, 96 * kk)
                    out, bias = (q_hi, bq) if name == "pq" else (k_hi, bk)
                    hi(part, b, g, name, out[:, :], bias[:, gg:gg + 1])
                elif name == "tu":
                    hi(part, b, g, name, e_hi[npar][:, :])
                elif name == "tr":
                    if part != "prologue":
                        act.wait_ge(xtop_ready, nb)
                    hi(part, b, g, name, x_hi[:, :])
                elif name in ("aq", "ak", "av"):
                    act.wait_ge(dense_full, number(part, b, g, name))
                    for dst in range(2):
                        for h in range(2):
                            to, rows, cols = a_parts(dst, h)
                            last = act.copy(a_hi[name[1]][to, cols], ps_dense[bank_of(part, g, name)][rows, 0:S // 2])
                    last.then_inc(hi_ready, 1)
                elif name == "mt":
                    if part != "prologue":
                        act.wait_ge(m_loaded, 32 * (GROUPS * b + g + 1))
                    hi(part, b, g, name, m_parts[0:GH, :])
                elif name[0] == "v":
                    tt = int(name[1])
                    if part != "first":
                        act.wait_ge(pv_done, NT * GROUPS * b - NT + tt + 1)
                    act.wait_ge(dense_full, number(part, b, g, name))
                    bank = bank_of(part, g, name)
                    act.copy(v_sb[:, tt, :], ps_dense[bank][:, :]).then_inc(dense_done[bank], 1)
                elif name == "den":
                    inverse_den(part, b, g)

            def inverse_den(part, b, g):
                k = STEPS - 1 if part == "epilogue" else GROUPS * b + g - 1
                if not (isinstance(k, int) and k == 0):
                    act.wait_ge(olo_done, k)
                act.wait_ge(dense_full, number(part, b, g, "den"))
                bank = bank_of(part, g, "den")
                act.activation(o_sb[:, :], ps_dense[bank][:, :], ACT.Ln).then_inc(dense_done[bank], 1)
                wait_done(act, part, b, g, "den")
                act.activation(o_sb[:, :], o_sb[:, :], ACT.Exp, scale=-1.0).then_inc(rden, 1)

            def rsqrt(nb):
                act.wait_ge(ln1, 10 * nb + 5)
                act.activation(ln1v[:, :], ve1[:, :], ACT.Ln).then_inc(rsq, 1)
                act.wait_ge(rsq, 2 * nb + 1)
                act.activation(y1[:, :], ln1v[:, :], ACT.Exp, scale=-0.5).then_inc(rsq, 1)

            def copy_raw(k, first):
                act.wait_ge(pv_done, NT * (k + 1))
                if not first:
                    act.wait_ge(o_scaled, k)
                act.copy(o_raw[:, :], ps_o[:, :]).then_inc(raw_copied, 1)

            def o_hi_part(part, b, g, k, gk):
                act.wait_ge(o_scaled, k + 1)
                if g == 1 and part in ("mid", "last"):
                    act.wait_ge(dense_full, number(part, b, 1, "wo3"))
                act.activation(o_hi[:, gk, :], o_sb[:, :], ACT.Identity, bias=bv[:, gk:gk + 1]).then_inc(ohi_done, 1)

            def center(part, b, pb_, st):
                act.wait_ge(ln2, 17 * pb_ + 4 * st + 3)
                act.wait_ge(xc_stored[st % 2], 16 + 16 * (NT // 2 * pb_ + st // 2))
                bank = bank_of(part, wo_group(part, st), f"wo{st}")
                act.activation(xc[:, st % 2, :], ps_dense[bank][:, :], ACT.Identity, bias=negm[:, st:st + 1]).then_inc(dense_done[bank], 1)

            def exp_unit(k, i, first):
                tt, j = i // GH, i % GH
                act.wait_ge(s2_full, UNITS * k + i + 1)
                if j == 0 and tt < NT - 1 and not first:
                    act.wait_ge(added, 3 * (k - 1) + tt + 1)
                act.activation(probs[:, tt, j, :], ps_s2[:, s2_bank(i), :], ACT.Exp).then_inc(exp_done, 1)

            for g, _, name in PROLOGUE:
                if name == "aq":
                    act.wait_ge(wo_loaded, 16)
                    act.copy(wo_hi[:, :, :], wo_stage).then_inc(wo_ready, 1)
                    act.wait_ge(loaded, 16 * LOADS)
                    act.copy(bo_stk[0:E_DIM, :], o_raw[0:E_DIM, :])
                    act.copy(o_hi[E_DIM:P, 0, :], o_raw[E_DIM:P, :]).then_inc(bo_ready, 1)
                dense("prologue", 0, 0, g, name)
                if name == "h0_3":
                    rsqrt(0)

            def batch(part, b, parity):
                for g in range(GROUPS):
                    k = GROUPS * b + g
                    start = part == "first" and g == 0
                    for i in range(UNITS):
                        for name in items_at(part, g, i):
                            dense(part, b, parity, g, name)
                        if i == 4 and not start:
                            copy_raw(k - 1, part == "first" and g == 1)
                        if i == DEN + 2 and not start:
                            o_hi_part(part, b, g, k - 1, g - 1 if g else GROUPS - 1)
                        if g == 1 and i == 14 and part != "last":
                            rsqrt(b + 1)
                        if part != "first":
                            for st, at in enumerate(CENTER_AT):
                                if at == (g, i):
                                    center(part, b, b - 1, st)
                        exp_unit(k, i, start)

            act.wait_ge(w_ready, 2)
            act.wait_ge(wo_ready, 2)
            act.wait_ge(bo_ready, 2)
            for_batches(act, batch)
            copy_raw(STEPS - 1, False)
            inverse_den("epilogue", B - 1, 0)
            o_hi_part("epilogue", B - 1, 0, STEPS - 1, GROUPS - 1)
            for st in range(NT):
                center("epilogue", B - 1, B - 1, st)

        @block.vector
        def _(dve):
            dve.memset(ones_mean[:, :], 1.0 / S).then_inc(consts, 1)
            dve.memset(ones_den[:, :], 1.0).then_inc(consts, 1)
            dve.memset(mean_64[:, :].bitcast(F32), 1.0 / E_DIM).then_inc(consts, 1)
            dve.wait_ge(rot_loaded, 16 * ROT_LOADS)
            two_pi = 6.283185307179586
            c1 = 6.28125
            c2 = 507.0 / 2 ** 18
            c3 = two_pi - c1 - c2
            chain = [0]

            def link(ins):
                chain[0] += 1
                ins.then_inc(trig_dve, 1)
                dve.wait_ge(trig_dve, chain[0])

            for out, phase, shift in ((cosr, 0.25, two_pi / 4), (sinr, 0.0, 0.0)):
                link(dve.tensor_scalar(turn, rot, 1.0 / two_pi, phase, ALU.mult, ALU.add))
                link(dve.tensor_scalar(red, turn, MAGIC, None, ALU.add))
                link(dve.tensor_scalar(turn, red, MAGIC, None, ALU.subtract))
                link(dve.scalar_tensor_tensor(red, turn, -c1, rot, ALU.mult, ALU.add))
                link(dve.scalar_tensor_tensor(out, turn, -c2, red, ALU.mult, ALU.add))
                link(dve.scalar_tensor_tensor(red, turn, -c3, out, ALU.mult, ALU.add))
                link(dve.tensor_scalar(turn, red, shift, 3.1415925, ALU.add, ALU.min))
                dve.tensor_scalar(out, turn, -3.1415925, None, ALU.max).then_inc(trig, 1)
                dve.wait_ge(trig, 1 if out is cosr else 2)
            dve.wait_ge(trig_act, 1)
            link(dve.scalar_tensor_tensor(red, cosr, float(DH) ** -0.5, spiral, ALU.mult, ALU.mult))

            def scale_weights(n, scale, bias, at):
                dve.wait_ge(trig_act, 2)
                dve.wait_ge(loaded, 16 * LOADS)
                dve.tensor_tensor(bias[:, :], bias_in[:, at:at + GROUPS], scale[:, S:L], ALU.mult)
                dve.tensor_tensor(w_in[n][:, :, :], w_in[n][:, :, :],
                                  scale[:, 0:S].unsqueeze(1).to_broadcast([P, NT, S]), ALU.mult).then_inc(w_ready, 1)

            def lo(part, b, g, name, out, hi_tile, bias=None, rows=slice(0, P)):
                dve.wait_ge(hi_ready, hi_number(part, b, g, name))
                bank = bank_of(part, g, name)
                src = ps_dense[bank][rows, :]
                if bias is None:
                    dve.tensor_tensor(out, src, hi_tile.bitcast(F32), ALU.subtract).then_inc(dense_done[bank], 1)
                else:
                    dve.scalar_tensor_tensor(out, src, bias, hi_tile.bitcast(F32), ALU.add, ALU.subtract).then_inc(dense_done[bank], 1)

            def dense(part, b, parity, g, name):
                nb, npar = (0, 0) if part == "prologue" else (b + 1, 1 - parity)
                bank = bank_of(part, g, name)
                ps_d = ps_dense[bank]
                if name in ("pq", "pk"):
                    gg = g if part == "prologue" else (g + 2) % GROUPS
                    hi_t, lo_t, bias = (q_hi, q_lo, bq) if name == "pq" else (k_hi, k_lo, bk)
                    lo(part, b, g, name, lo_t[:, :], hi_t[:, :], bias[:, gg:gg + 1])
                elif name == "tu":
                    lo(part, b, g, name, e_lo[npar][:, :], e_hi[npar][:, :])
                elif name == "tr":
                    lo(part, b, g, name, x_stk[E_DIM:P, :], x_hi[E_DIM:P, :], rows=slice(E_DIM, P))
                elif name in ("aq", "ak", "av"):
                    dve.wait_ge(hi_ready, hi_number(part, b, g, name))
                    for dst in range(2):
                        for h in range(2):
                            to, rows, cols = a_parts(dst, h)
                            last = dve.tensor_tensor(a_lo[name[1]][to, cols], ps_d[rows, 0:S // 2],
                                                     a_hi[name[1]][rows, cols].bitcast(F32), ALU.subtract)
                    last.then_inc(dense_done[bank], 1)
                elif name == "mt":
                    lo(part, b, g, name, m_parts[DH:DH + GH, :], m_parts[0:GH, :], rows=slice(0, GH))
                elif name == "mean":
                    dve.wait_ge(dense_full, number(part, b, g, name))
                    dve.tensor_tensor(cent[:, :, :], emb[:, :, :], ps_d[:, 0:E_DIM].unsqueeze(1).to_broadcast([P, NT, E_DIM]),
                                      ALU.subtract).then_inc(dense_done[bank], 1)
                elif name.startswith("h0_"):
                    st = int(name[3])
                    dve.wait_ge(dense_full, number(part, b, g, name))
                    dve.bn_stats(bn1[:, st, :], ps_d[:, :]).then_inc(dense_done[bank], 1)
                    if st == NT - 1:
                        variance(part, b, g, nb)
                elif name in WO:
                    h1_rows(ps_d, part, b, g, int(name[2]))

            def variance(part, b, g, nb):
                wait_done(dve, part, b, g, "h0_3")
                stand_alone(dve, dve_waited)
                for st in range(NT):
                    dve.bn_aggr(mv1[:, st, :], bn1[:, st, :]).then_inc(ln1, 1)
                dve.wait_ge(ln1, 10 * nb + 4)
                dve.tensor_scalar(ve1[:, :], mv1[:, :, 1], EPS, None, ALU.add).then_inc(ln1, 1)

            def newton(nb):
                dve.wait_ge(rsq, 2 * (nb + 1))
                dve.tensor_tensor(t1[:, :], y1[:, :], y1[:, :], ALU.mult).then_inc(ln1, 1)
                dve.wait_ge(ln1, 10 * nb + 6)
                dve.tensor_tensor(ln1v[:, :], t1[:, :], ve1[:, :], ALU.mult).then_inc(ln1, 1)
                dve.wait_ge(ln1, 10 * nb + 7)
                dve.tensor_scalar(t1[:, :], ln1v[:, :], -0.5, 1.5, ALU.mult, ALU.add).then_inc(ln1, 1)
                dve.wait_ge(ln1, 10 * nb + 8)
                dve.scalar_tensor_tensor(r8[:, :], y1[:, :], 0.125, t1[:, :], ALU.mult, ALU.mult).then_inc(ln1, 1)
                dve.wait_ge(ln1, 10 * nb + 9)
                dve.tensor_tensor(emb2[:, :, :, :], emb[:, :, :].unsqueeze(2).to_broadcast([P, NT, 2, E_DIM]),
                                  r8[:, :].unsqueeze(2).unsqueeze(2).to_broadcast([P, NT, 2, E_DIM]),
                                  ALU.mult).then_inc(ln1, 1)

            def row_max(k, g, u):
                dve.wait_ge(s1_full, UNITS * k + u + 1)
                j, st = u // NT, u % NT
                dve.tensor_reduce(negmax[:, g % 2, st, j:j + 1], ps_s1[:, u % 2, :], AX_X, ALU.max, negate=True).then_inc(max_done, 1)

            def scale_o(k):
                dve.wait_ge(rden, k + 1)
                dve.wait_ge(raw_copied, k + 1)
                dve.tensor_tensor(o_sb[:, :], o_raw[:, :], o_sb[:, :], ALU.mult).then_inc(o_scaled, 1)

            def o_lo_part(k, gk):
                dve.wait_ge(ohi_done, k + 1)
                dve.scalar_tensor_tensor(o_lo[:, gk, :], o_sb[:, :], bv[:, gk:gk + 1], o_hi[:, gk, :].bitcast(F32),
                                         ALU.add, ALU.subtract).then_inc(olo_done, 1)

            def h1_rows(ps_d, part, b, g, st):
                pb_ = B - 1 if part == "epilogue" else b - 1
                if st:
                    centered_max(part, b, pb_, st - 1)
                dve.wait_ge(dense_full, number(part, b, g, f"wo{st}"))
                dve.bn_stats(bn2[:, :], ps_d[:, :]).then_inc(ln2, 1)
                dve.wait_ge(ln2, 17 * pb_ + 4 * st + 1)
                stand_alone(dve, dve_waited)
                dve.bn_aggr(mv2[:, st, 0:2], bn2[:, :]).then_inc(ln2, 1)
                dve.wait_ge(ln2, 17 * pb_ + 4 * st + 2)
                dve.tensor_scalar(negm[:, st:st + 1], mv2[:, st, 0:1], -1.0, None, ALU.mult).then_inc(ln2, 1)

            def centered_max(part, b, pb_, st):
                wait_done(dve, part, b, wo_group(part, st), f"wo{st}")
                dve.tensor_reduce(mv2[:, st, 2:3], xc[:, st % 2, :], AX_X, ALU.max, apply_absolute_value=True).then_inc(ln2, 1)

            def keep_stats(pb_):
                dve.wait_ge(ln2, 17 * pb_ + 16)
                dve.tensor_copy(stats[:, bass.ds(12 * pb_, 12)], mv2[:, :, :].rearrange("p t c -> p (t c)")).then_inc(ln2, 1)

            for g, _, name in PROLOGUE:
                if (g, name) == (1, "pq"):
                    dve.wait_ge(wo_loaded, 16)
                    dve.wait_ge(wo_ready, 1)
                    dve.tensor_tensor(wo_lo[:, :, :], wo_stage, wo_hi[:, :, :].bitcast(F32), ALU.subtract).then_inc(wo_ready, 1)
                    dve.wait_ge(bo_ready, 1)
                    dve.tensor_tensor(bo_stk[E_DIM:P, :], o_raw[E_DIM:P, :], o_hi[E_DIM:P, 0, :].bitcast(F32),
                                      ALU.subtract).then_inc(bo_ready, 1)
                if name == "tr":
                    newton(0)
                    scale_weights("q", red, bq, 0)
                if name == "aq":
                    scale_weights("k", sinr, bk, GROUPS)
                if name == "mt":
                    for u in range(UNITS):
                        row_max(0, 0, u)
                dense("prologue", 0, 0, g, name)
            for u in range(AHEAD):
                row_max(1, 1, u)

            def batch(part, b, parity):
                for g in range(GROUPS):
                    k = GROUPS * b + g
                    start = part == "first" and g == 0
                    for i in range(UNITS):
                        u = i + AHEAD
                        if u < UNITS and not (part == "last" and g + 1 >= GROUPS):
                            row_max(k + 1, (g + 1) % GROUPS, u)
                        if u >= UNITS and not (part == "last" and g + 2 >= GROUPS):
                            row_max(k + 2, (g + 2) % GROUPS, u - UNITS)
                        for name in items_at(part, g, i):
                            dense(part, b, parity, g, name)
                        if i == DEN + 1 and not start:
                            scale_o(k - 1)
                        if i == DEN + 3 and not start:
                            o_lo_part(k - 1, g - 1 if g else GROUPS - 1)
                        if g == 1 and i == 14 and part != "last":
                            newton(b + 1)
                        if g == 1 and i == 8 and part != "first":
                            centered_max(part, b, b - 1, NT - 1)
                            keep_stats(b - 1)

            for_batches(dve, batch)
            dve.wait_ge(pv_done, NT * STEPS)
            dve.wait_ge(added, 3 * STEPS - 1)
            dve.tensor_tensor(probs[:, NT - 1, :, :], probs[:, NT - 2, :, :], probs[:, NT - 1, :, :], ALU.add).then_inc(added, 1)
            scale_o(STEPS - 1)
            o_lo_part(STEPS - 1, GROUPS - 1)
            for st in range(NT):
                dense("epilogue", B - 1, 1, 0, f"wo{st}")
            centered_max("epilogue", B - 1, B - 1, NT - 1)
            keep_stats(B - 1)

        @block.gpsimd
        def _(pool):
            pool.memset(ident[:, :], 0.0).then_inc(pool_const, 1)
            pool.wait_ge(pool_const, 1)
            pool.affine_select(out=ident[:, :], in_=ident[:, :], compare_op=ALU.not_equal, fill=1.0, base=0,
                               pattern=[[-1, P]], channel_multiplier=1).then_inc(pool_const, 1)

            def gather(nb, first):
                pool.wait_ge(ids_loaded, 16 * (nb + 1))
                if not first:
                    pool.wait_ge(ln1, 10 * nb)
                    pool.wait_ge(emb2_ready, nb)
                    stand_alone(pool, pool_waited)
                for tt in range(NT):
                    pool.indirect_dma_start(emb[:, tt, :], None, d["table"],
                                            bass.IndirectOffsetOnAxis(ap=ids[:, tt:tt + 1].bitcast(U32), axis=0)).then_inc(gathered, 16)

            def double(part, b, nb, first):
                pool.wait_ge(gathered, 16 * NT * (nb + 1))
                if not first:
                    if part == "first":
                        pool.wait_ge(dense_full, number("prologue", 0, 0, "tr"))
                    else:
                        pool.wait_ge(dense_full, number("mid", b - 1, 2, "tr"))
                stand_alone(pool, pool_waited)
                pool.tensor_scalar(emb2[:, :, :, :], emb[:, :, :].unsqueeze(2).to_broadcast([P, NT, 2, E_DIM]),
                                   1.0, 0.0, ALU.mult, ALU.add).then_inc(emb2_ready, 1)

            def stack_e(part, b, g, nb, par):
                pool.wait_ge(hi_ready, hi_number(part, b, g, "tu"))
                stand_alone(pool, pool_waited)
                pool.tensor_scalar(e_stk8[par][0:E_DIM, :], e_hi[par][0:E_DIM, :].bitcast(F32), 0.125, 0.0,
                                   ALU.mult, ALU.add).then_inc(stk8_ready, 1)
                wait_done(pool, part, b, g, "tu")
                pool.wait_ge(stk8_ready, 2 * nb + 1)
                if part != "prologue":
                    pool.wait_ge(added, 3 * (GROUPS * b + 1))
                stand_alone(pool, pool_waited)
                pool.tensor_scalar(e_stk8[par][E_DIM:P, :], e_lo[par][E_DIM:P, :].bitcast(F32), 0.125, 0.0,
                                   ALU.mult, ALU.add).then_inc(stk8_ready, 1)
                pool.wait_ge(stk8_ready, 2 * (nb + 1))

            def stack_x(part, b, g, nb):
                pool.wait_ge(hi_ready, hi_number(part, b, g, "tr"))
                stand_alone(pool, pool_waited)
                pool.tensor_scalar(x_stk[0:E_DIM, :], x_hi[0:E_DIM, :].bitcast(F32), 1.0, 0.0,
                                   ALU.mult, ALU.add).then_inc(xtop_ready, 1)

            def add(k, a):
                pool.wait_ge(pv_done, NT * k + a + 2)
                if a:
                    pool.wait_ge(added, 3 * k + a)
                pool.tensor_tensor(probs[:, a + 1, :, :], probs[:, a, :, :], probs[:, a + 1, :, :], ALU.add).then_inc(added, 1)

            gather(0, True)
            pool.wait_ge(pool_const, 2)
            for slot in range(GROUPS):
                pool.memset(k_stack[slot][QK_ROWS:QKM_ROWS, :, :].bitcast(F32), 1.0).then_inc(pool_const, 1)
            pool.wait_ge(pool_const, 2 + GROUPS)
            double("prologue", 0, 0, True)
            stack_e("prologue", 0, 0, 0, 0)
            stack_x("prologue", 0, 0, 0)

            def batch(part, b, parity):
                for g in range(GROUPS):
                    k = GROUPS * b + g
                    if g == 2 and part != "last":
                        stack_x(part, b, g, b + 1)
                    if not (part == "first" and g == 0):
                        add(k - 1, 2)
                    if g == 1 and part != "last":
                        double(part, b, b + 1, False)
                    if g == 1 and part != "last":
                        stack_e(part, b, g, b + 1, 1 - parity)
                    add(k, 0)
                    add(k, 1)
                    if g == 0 and part != "last":
                        gather(b + 1, False)

            for_batches(pool, batch)


def linear_block(nc, d, xc_dram, stats, out):
    with ExitStack() as ctx:
        def sb(name, shape, dt=F32):
            return ctx.enter_context(nc.sbuf_tensor("lin_" + name, shape, dt))

        def pb(name, shape, dt=F32):
            return ctx.enter_context(nc.psum_tensor("lin_" + name, shape, dt))

        def sem(name):
            return ctx.enter_context(nc.semaphore("lin_" + name))

        TILES = B * NT
        BUFS = 4
        wf = sb("wf", [P, NT, S])
        wf_y, wf_c = sb("wf_y", [P, NT, S]), sb("wf_c", [P, NT, S])
        wf_q = sb("wf_q", [P, NT, S], BF16)
        fb = sb("fb", [P, S])
        fb_r = sb("fb_r", [P, S])
        fb_h = sb("fb_h", [P, S], BF16)
        fb3 = sb("fb3", [3 * DH, S], BF16)
        sel3 = sb("sel3", [3 * DH, P], BF16)
        identb = sb("identb", [P, P], BF16)
        row = {n: sb(n, [P, TILES]) for n in ("f_ve", "f_ln", "f_y", "f_t", "f_t2", "f_r")}
        a_mean = sb("a_mean", [P, B, 2, NT])
        cur = sb("cur", [P, BUFS, 2, NT])
        am, amr = sb("am", [P, 2]), sb("amr", [P, 2])
        sc = sb("sc", [P, 8])
        x = [sb(f"x{i}", [P, NT, S]) for i in range(BUFS)]
        y = [sb(f"y{i}", [P, NT, S]) for i in range(2)]
        c = [sb(f"c{i}", [P, NT, S]) for i in range(2)]
        q = [sb(f"q{i}", [P, NT, S], BF16) for i in range(2)]
        qt = [sb(f"qt{i}", [P, NT, S], BF16) for i in range(2)]
        o = [sb(f"o{i}", [P, NT, S]) for i in range(2)]
        ps_t = pb("ps_t", [P, NT, 2 * S], BF16)
        ps_f = pb("ps_f", [P, NT, S])

        w_loaded, fb_loaded = sem("w_loaded"), sem("fb_loaded")
        x_loaded = [sem(f"x_loaded{i}") for i in range(BUFS)]
        f_const = sem("f_const")
        f_dve, f_act, f_pool = sem("f_dve"), sem("f_act"), sem("f_pool")
        wq_done = sem("wq_done")
        set_up = sem("set_up")
        scales_ready = sem("scales_ready")
        cur_ready = sem("cur_ready")
        y_ready = sem("y_ready")
        r_ready = sem("r_ready")
        masked = sem("masked")
        c_ready = sem("c_ready")
        rounded = sem("rounded")
        q_ready = sem("q_ready")
        turned = sem("turned")
        qt_ready = sem("qt_ready")
        f_full = sem("f_full")
        o_ready = sem("o_ready")
        stored = [sem(f"stored{i}") for i in range(2)]

        def iterations(eng, body, first=0):
            for it in range(first, 4):
                body(it, it)
            with eng.Fori(1, B // 4 - 1) as four:
                i = eng.snap(four * 4)
                for m in range(4):
                    body(i + m, 4 + m, True)
            for it in range(B - 4, B + 2):
                body(it, it)

        def half(t, h):
            return t[:, h * NT // 2:(h + 1) * NT // 2, :]

        def stages(it, m, mid):
            return [(it - n if mid or 0 <= it - n < B else None) for n in range(3)]

        block = ctx.enter_context(nc.Block())

        @block.sync
        def _(sp):
            sp.dma_start(wf[:, :, :], d["wf"].rearrange("(t p) n -> p t n", p=P)).then_inc(w_loaded, 16)
            sp.dma_start(fb[:, :], d["fb_row"].partition_broadcast(P).rearrange("p a n -> p (a n)")).then_inc(fb_loaded, 16)

            def load(b, i, n):
                sp.dma_start(x[i][:, :, :], xc_dram[b].rearrange("t p n -> p t n")).then_inc(x_loaded[i], 16)

            load(0, 0, 0)
            load(1, 1, 0)

            def body(it, m, mid=False):
                a, _, cc = stages(it, m, mid)
                if mid or it + 2 < B:
                    if mid or it + 2 >= BUFS:
                        sp.wait_ge(o_ready, NT * (it - 1))
                    load(it + 2, (m + 2) % BUFS, 0)
                if cc is not None:
                    sp.wait_ge(o_ready, NT * (cc + 1))
                    sp.dma_start(out[cc].rearrange("(t p) n -> p t n", p=P), o[m % 2][:, :, :]).then_inc(stored[m % 2], 16)

            iterations(sp, body)
            for i in range(2):
                sp.wait_ge(stored[i], 16 * B // 2)

        @block.scalar
        def _(act):
            act.wait_ge(f_dve, 1)
            act.activation(row["f_ln"][:, :], row["f_ve"][:, :], ACT.Ln).then_inc(f_act, 1)
            act.wait_ge(f_act, 1)
            act.activation(row["f_y"][:, :], row["f_ln"][:, :], ACT.Exp, scale=-0.5).then_inc(f_act, 1)
            act.wait_ge(scales_ready, 1)
            for t in range(NT):
                last = act.activation(wf_y[:, t, :], wf[:, t, :], ACT.Identity, scale=sc[:, 3:4])
            last.then_inc(f_act, 1)

            def body(it, m, mid=False):
                a, bb, _ = stages(it, m, mid)
                if a is not None:
                    act.wait_ge(x_loaded[m % BUFS], 16 * ((it - m % BUFS) // BUFS + 1) if not mid else x_count(it, m))
                    act.wait_ge(cur_ready, it + 1)
                    if mid or it >= 2:
                        act.wait_ge(q_ready, 2 * (it - 1))
                    for st in range(NT):
                        act.activation(y[m % 2][:, st, :], x[m % BUFS][:, st, :], ACT.Identity,
                                       scale=cur[:, m % BUFS, 0, st:st + 1]).then_inc(y_ready, 1)
                if bb is not None:
                    for st in range(NT):
                        act.wait_ge(turned, NT * bb + st + 1)
                        if st == 0 and (mid or bb >= 2):
                            act.wait_ge(f_full, NT * (bb - 1))
                        act.copy(qt[(m + 1) % 2][:, st, :], ps_t[:, st, 0:S]).then_inc(qt_ready, 1)
                if a is not None:
                    act.wait_ge(y_ready, NT * (it + 1))
                    for st in range(NT):
                        act.activation(x[m % BUFS][:, st, :], x[m % BUFS][:, st, :], ACT.Identity,
                                       bias=cur[:, m % BUFS, 1, st:st + 1]).then_inc(r_ready, 1)

            def x_count(it, m):
                return (it - m % BUFS) * (16 // BUFS) + 16

            iterations(act, body)

        @block.vector
        def _(dve):
            steps = [0]

            def link(ins):
                steps[0] += 1
                ins.then_inc(f_dve, 1)
                dve.wait_ge(f_dve, steps[0])

            st3 = stats[:, :].rearrange("p (t c) -> p t c", c=3)
            link(dve.tensor_scalar(row["f_ve"][:, :], st3[:, :, 1], EPS, None, ALU.add))
            dve.memset(identb[:, :], 0.0).then_inc(f_const, 1)
            link(dve.memset(sel3[:, :], 0.0))
            for i in range(3):
                link(dve.memset(sel3[i * DH:i * DH + 1, :], 1.0))
            dve.wait_ge(f_act, 2)
            link(dve.tensor_tensor(row["f_t"][:, :], row["f_y"][:, :], row["f_y"][:, :], ALU.mult))
            link(dve.tensor_tensor(row["f_t2"][:, :], row["f_t"][:, :], row["f_ve"][:, :], ALU.mult))
            link(dve.tensor_scalar(row["f_t"][:, :], row["f_t2"][:, :], -0.5, 1.5, ALU.mult, ALU.add))
            link(dve.tensor_tensor(row["f_r"][:, :], row["f_y"][:, :], row["f_t"][:, :], ALU.mult))
            link(dve.tensor_tensor(row["f_t"][:, :], row["f_r"][:, :], st3[:, :, 2], ALU.mult))
            link(dve.tensor_reduce(am[:, 0:1], row["f_t"][:, :], AX_X, ALU.max))
            dve.wait_ge(w_loaded, 16)
            link(dve.tensor_reduce(am[:, 1:2], wf[:, :, :].rearrange("p t n -> p (t n)"), AX_X, ALU.max, apply_absolute_value=True))
            dve.tensor_copy(amr[:, :], am[:, :]).then_inc(set_up, 1)
            dve.wait_ge(f_pool, 3)
            link(dve.tensor_scalar(sc[:, 0:1], amr[:, 0:1], 1.0 / FP8_RANGE, None, ALU.mult))
            link(dve.tensor_tensor(sc[:, 6:7], amr[:, 0:1], amr[:, 1:2], ALU.max))
            link(dve.tensor_scalar(sc[:, 1:2], sc[:, 6:7], 1.0 / FP8_RANGE, None, ALU.mult))
            dve.reciprocal(sc[:, 2:4], sc[:, 0:2]).then_inc(scales_ready, 1)
            link(dve.tensor_tensor(sc[:, 4:5], sc[:, 0:1], sc[:, 1:2], ALU.mult))
            link(dve.reciprocal(sc[:, 5:6], sc[:, 4:5]))
            link(dve.tensor_scalar(a_mean[:, :, 0, :], row["f_r"][:, :].rearrange("p (b t) -> p b t", t=NT), sc[:, 2:3], None, ALU.mult))
            link(dve.tensor_copy(a_mean[:, :, 1, :], st3[:, :, 0].rearrange("p (b t) -> p b t", t=NT)))

            def mask(out, src):
                return dve.tensor_scalar(out.bitcast(U32), src.bitcast(U32), 0x7F800000, None, ALU.bitwise_and)

            def shifter(out, src):
                return dve.tensor_scalar(out, src, 2.0 ** -6, 1.5 * 2.0 ** 20, ALU.max, ALU.mult)

            def set_current(it, m):
                dve.tensor_copy(cur[:, m % BUFS, :, :].rearrange("p c t -> p (c t)"),
                                a_mean[:, :, :, :].rearrange("p b c t -> p (b c t)")[:, bass.ds(2 * NT * it, 2 * NT)]).then_inc(cur_ready, 1)

            set_current(0, 0)
            dve.wait_ge(fb_loaded, 16)
            link(dve.tensor_scalar(fb_r[:, :], fb[:, :], sc[:, 5:6], None, ALU.mult))
            link(dve.tensor_copy(fb_h[:, :], fb_r[:, :]))
            link(dve.tensor_copy(fb3[0:DH, :], fb_r[0:DH, :]))
            link(dve.tensor_tensor(fb[:, :], fb_r[:, :], fb_h[:, :], ALU.subtract))
            dve.wait_ge(f_act, 3)
            link(mask(wf_c[:, :, :], wf_y[:, :, :]))
            link(shifter(wf_c[:, :, :], wf_c[:, :, :]))
            def body(it, m, mid=False):
                a, bb, cc = stages(it, m, mid)
                if a is not None and (mid or it > 0):
                    set_current(it, m)
                if bb is not None:
                    for h in range(2):
                        dve.wait_ge(rounded, 2 * bb + h + 1)
                        if h == 0 and (mid or bb >= 2):
                            dve.wait_ge(turned, NT * (bb - 1))
                        dve.tensor_tensor(half(q[(m + 1) % 2], h), half(y[(m + 1) % 2], h), half(c[(m + 1) % 2], h),
                                          ALU.subtract).then_inc(q_ready, 1)
                if a is not None:
                    for h in range(2):
                        dve.wait_ge(y_ready, NT * it + NT // 2 * (h + 1))
                        if h == 0 and (mid or it >= 2):
                            dve.wait_ge(q_ready, 2 * (it - 1))
                        mask(half(c[m % 2], h), half(y[m % 2], h)).then_inc(masked, 1)
                    for h in range(2):
                        dve.wait_ge(masked, 2 * it + h + 1)
                        shifter(half(c[m % 2], h), half(c[m % 2], h)).then_inc(c_ready, 1)
                if cc is not None:
                    for st in range(NT):
                        dve.wait_ge(f_full, NT * cc + st + 1)
                        if st == 0:
                            dve.wait_ge(r_ready, NT * (cc + 1))
                            if mid or cc >= 2:
                                dve.wait_ge(stored[m % 2], 8 * (cc - m % 2))
                        dve.scalar_tensor_tensor(o[m % 2][:, st, :], ps_f[:, st, :], sc[:, 4:5], x[(m - 2) % BUFS][:, st, :],
                                                 ALU.mult, ALU.add).then_inc(o_ready, 1)

            body(0, 0)
            link(dve.tensor_tensor(wf_y[:, :, :], wf_y[:, :, :], wf_c[:, :, :], ALU.add))
            link(dve.tensor_tensor(wf_q[:, :, :], wf_y[:, :, :], wf_c[:, :, :], ALU.subtract))
            link(dve.tensor_copy(fb3[DH:2 * DH, :], fb[DH:2 * DH, :]))
            link(dve.tensor_copy(fb_h[:, :], fb[:, :]))
            link(dve.tensor_tensor(fb_r[:, :], fb[:, :], fb_h[:, :], ALU.subtract))
            dve.tensor_copy(fb3[2 * DH:3 * DH, :], fb_r[2 * DH:3 * DH, :]).then_inc(wq_done, 1)
            iterations(dve, body, 1)

        @block.gpsimd
        def _(pool):
            pool.wait_ge(f_const, 1)
            pool.affine_select(out=identb[:, :], in_=identb[:, :], compare_op=ALU.not_equal, fill=1.0, base=0,
                               pattern=[[-1, P]], channel_multiplier=1).then_inc(f_pool, 1)
            pool.wait_ge(set_up, 1)
            pool.partition_all_reduce(amr[:, 0:1], am[:, 0:1], P, bass.bass_isa.ReduceOp.max).then_inc(f_pool, 1)
            pool.partition_all_reduce(amr[:, 1:2], am[:, 1:2], P, bass.bass_isa.ReduceOp.max).then_inc(f_pool, 1)

            def body(it, m, mid=False):
                a, _, _ = stages(it, m, mid)
                if a is not None:
                    for h in range(2):
                        pool.wait_ge(c_ready, 2 * it + h + 1)
                        pool.tensor_tensor(half(y[m % 2], h), half(y[m % 2], h), half(c[m % 2], h), ALU.add).then_inc(rounded, 1)

            iterations(pool, body)

        @block.tensor
        def _(pe):
            pe.wait_ge(f_pool, 1)
            pe.wait_ge(wq_done, 1)

            def body(it, m, mid=False):
                _, bb, _ = stages(it, m, mid)
                if bb is None:
                    return
                for st in range(NT):
                    if st % (NT // 2) == 0:
                        pe.wait_ge(q_ready, 2 * bb + st // (NT // 2) + 1)
                    if mid or bb >= 1:
                        pe.wait_ge(qt_ready, NT * (bb - 1) + st + 1)
                    for ib in range(NT):
                        last = pe.transpose(ps_t[:, st, ib * P:(ib + 1) * P], q[(m + 1) % 2][:, st, ib * P:(ib + 1) * P], identb[:, :])
                    last.then_inc(turned, 1)
                for st in range(NT):
                    pe.wait_ge(qt_ready, NT * bb + st + 1)
                    if mid or bb >= 1:
                        pe.wait_ge(o_ready, NT * (bb - 1) + st + 1)
                    pe.matmul(ps_f[:, st, :], sel3[:, :], fb3[:, :], start=True, stop=False)
                    for ib in range(NT):
                        last = pe.matmul(ps_f[:, st, :], qt[(m + 1) % 2][:, st, ib * P:(ib + 1) * P], wf_q[:, ib, :],
                                         start=False, stop=(ib == NT - 1))
                    last.then_inc(f_full, 1)

            iterations(pe, body)


def tower(nc, d, out):
    with ExitStack() as ctx:
        stats = ctx.enter_context(nc.sbuf_tensor("stats", [P, B * NT * 3], F32))
        xc_dram = nc.dram_tensor("xc_dram", (B, NT, P, S), F32, kind="Internal").ap()
        attention_block(nc, d, xc_dram, stats)
        linear_block(nc, d, xc_dram, stats, out)


def kernel(**inputs):
    import numpy as np
    from concourse import bacc
    from concourse.bass_utils import run_bass_kernel_spmd

    nc = bacc.Bacc("TRN2", target_bir_lowering=False, num_devices=1, dynamic_dma_scratch_size=4096)
    a = {n: np.asarray(v) for n, v in inputs.items()}

    def by_dim(v):
        return v.reshape((GROUPS, GH, DH) + v.shape[1:]).swapaxes(1, 2).reshape(v.shape)

    def cols(v):
        return v.reshape(GROUPS, P).T

    rot = by_dim(a["L0_attn_helix_rotation"])
    spiral = by_dim(np.repeat(a["L0_attn_spiral_weight"], DH))
    arrays = {
        "ids": a["x"].reshape(B, NT, P).swapaxes(1, 2),
        "table": a["L0_tok_weight"],
        "wq": by_dim(a["L0_attn_Wq"]).T, "wk": by_dim(a["L0_attn_Wk"]).T, "wv": a["L0_attn_Wv"].T,
        "wo": a["L0_attn_Wo"].T, "wf": a["L0_ffn_weight"].T,
        "bq_col": cols(by_dim(a["L0_attn_bq"])), "bk_col": cols(by_dim(a["L0_attn_bk"])), "bv_col": cols(a["L0_attn_bv"]),
        "bo_row": a["L0_attn_bo"][None], "fb_row": a["L0_ffn_bias"][None],
        "rot_row": rot[None], "rot_col": cols(rot), "spiral_row": spiral[None], "spiral_col": cols(spiral),
    }
    arrays = {f"in_{n}": np.ascontiguousarray(v) for n, v in arrays.items()}
    d = {n[3:]: nc.dram_tensor(n, v.shape, mybir.dt.from_np(v.dtype), kind="ExternalInput").ap() for n, v in arrays.items()}
    out = nc.dram_tensor("out", (B, S, S), F32, kind="ExternalOutput").ap()
    tower(nc, d, out)
    r = run_bass_kernel_spmd(nc, [arrays], core_ids=[0])
    return r.results[0]["out"]
```
